# Optimizing a Trainium2 kernel written in Bass

```python
import numpy as np
import jax
import jax.numpy as jnp

def _softmax(x, axis=-1):
    return jax.nn.softmax(x, axis=axis)

def _gelu(x):
    return jax.nn.gelu(x, approximate=True)

def _silu(x):
    return jax.nn.silu(x)

def _sigmoid(x):
    return jax.nn.sigmoid(x)

def _layernorm(x, axis=-1, eps=1e-05):
    m = jnp.mean(x, axis=axis, keepdims=True)
    v = jnp.var(x, axis=axis, keepdims=True)
    return (x - m) / jnp.sqrt(v + eps)

def _scatter_add(tgt, idx, src, axis=0):
    return tgt.at[idx].add(src)

def _segment_sum(src, seg, n):
    return jax.ops.segment_sum(src, seg, n)
kernel_name = 'mk_cond_seq_d4_seqx_r8_f13a5c'

def setup_inputs(seed: int=0):
    np.random.seed(seed)
    _w = jnp.asarray

    def _rec_inputs():
        import jax
        import jax.numpy as jnp
        _rk = jax.random.key(seed)
        x = -0.0003482 + 1 * jax.random.normal(jax.random.fold_in(_rk, 1), (2, 512, 144), jnp.float32)
        _lenS = 512 - jax.random.randint(jax.random.fold_in(_rk, 7), (2,), 0, max(1, 512 // 4) + 1, jnp.int32)
        _lenS2 = 512 - jax.random.randint(jax.random.fold_in(_rk, 8), (2,), 0, max(1, 512 // 4) + 1, jnp.int32)
        cond_1152 = -0.00342701 + 1.00097 * jax.random.normal(jax.random.fold_in(_rk, 11), (2, 144), jnp.float32)
        return (x, cond_1152)
    x, cond_1152 = _rec_inputs()

    def _L0_cond_setup():
        import jax, jax.numpy as jnp
        import numpy as np
        B, T, D, H = (64, 32, 144, 16)
        HD = D // H
        EPS = 1e-06

        def _ln(x):
            mu = jnp.mean(x, axis=-1, keepdims=True)
            var = jnp.var(x, axis=-1, keepdims=True)
            return (x - mu) * jax.lax.rsqrt(var + EPS)

        def _modulate(x, shift, scale):
            return x * (1.0 + scale[:, None, :]) + shift[:, None, :]

        def _attn(x, Wq, Wk, Wv, Wp, bp):
            b, t, d = x.shape
            q = (x @ Wq).reshape(b, t, H, HD).transpose(0, 2, 1, 3)
            k = (x @ Wk).reshape(b, t, H, HD).transpose(0, 2, 1, 3)
            v = (x @ Wv).reshape(b, t, H, HD).transpose(0, 2, 1, 3)
            scores = jnp.einsum('bhqd,bhkd->bhqk', q, k) / np.sqrt(HD)
            mask = jnp.triu(jnp.ones((t, t), bool), k=1)
            scores = jnp.where(mask, -jnp.inf, scores)
            w = jax.nn.softmax(scores, axis=-1)
            ctx = jnp.einsum('bhqk,bhkd->bhqd', w, v).transpose(0, 2, 1, 3).reshape(b, t, d)
            return ctx @ Wp + bp

        def _mlp(x, W1, b1, W2, b2):
            return jax.nn.silu(x @ W1 + b1) @ W2 + b2
        key = jax.random.key(seed)
        ks = jax.random.split(key, 12)
        s = lambda fan_in: 1.0 / np.sqrt(fan_in)
        return {'x': jax.random.normal(ks[0], (B, T, D), jnp.float32), 'c': jax.random.normal(ks[1], (B, D), jnp.float32), 'Wq': jax.random.normal(ks[2], (D, D), jnp.float32) * s(D), 'Wk': jax.random.normal(ks[3], (D, D), jnp.float32) * s(D), 'Wv': jax.random.normal(ks[4], (D, D), jnp.float32) * s(D), 'Wp': jax.random.normal(ks[5], (D, D), jnp.float32) * s(D), 'bp': jnp.zeros((D,), jnp.float32), 'W1': jax.random.normal(ks[6], (D, 4 * D), jnp.float32) * s(D), 'b1': jnp.zeros((4 * D,), jnp.float32), 'W2': jax.random.normal(ks[7], (4 * D, D), jnp.float32) * s(4 * D), 'b2': jnp.zeros((D,), jnp.float32), 'Wa': jax.random.normal(ks[8], (D, 6 * D), jnp.float32) * s(D), 'ba': jnp.zeros((6 * D,), jnp.float32)}
    _L0_cond_all = _L0_cond_setup()
    _L0_cond_in = {k: v for k, v in _L0_cond_all.items() if k in ('Wq', 'Wk', 'Wv', 'Wp', 'bp', 'W1', 'b1', 'W2', 'b2', 'Wa', 'ba')}
    del _L0_cond_all

    def _L1_cond_setup():
        import jax, jax.numpy as jnp
        import numpy as np
        B, N, D = (8, 128, 144)
        H = 16
        HD = D // H
        HID = 4 * D
        EPS = 1e-06

        def _ln(x):
            mu = jnp.mean(x, axis=-1, keepdims=True)
            var = jnp.mean(jnp.square(x - mu), axis=-1, keepdims=True)
            return (x - mu) * jax.lax.rsqrt(var + EPS)

        def _modulate(x, shift, scale):
            return x * (1.0 + scale[:, None, :]) + shift[:, None, :]

        def _attn(x, w_qkv, b_qkv, w_proj, b_proj):
            b, n, d = x.shape
            qkv = (x @ w_qkv + b_qkv).reshape(b, n, 3, H, HD)
            q = qkv[:, :, 0].transpose(0, 2, 1, 3)
            k = qkv[:, :, 1].transpose(0, 2, 1, 3)
            v = qkv[:, :, 2].transpose(0, 2, 1, 3)
            scores = jnp.einsum('bhnd,bhmd->bhnm', q, k) * HD ** (-0.5)
            attn = jax.nn.softmax(scores, axis=-1)
            out = jnp.einsum('bhnm,bhmd->bhnd', attn, v)
            out = out.transpose(0, 2, 1, 3).reshape(b, n, d)
            return out @ w_proj + b_proj
        key = jax.random.key(seed)
        ks = jax.random.split(key, 12)
        s = 0.02
        return {'x': jax.random.normal(ks[0], (B, N, D), jnp.float32), 't_emb': jax.random.normal(ks[1], (B, D), jnp.float32), 'w_qkv': jax.random.normal(ks[2], (D, 3 * D), jnp.float32) * s, 'b_qkv': jax.random.normal(ks[3], (3 * D,), jnp.float32) * s, 'w_proj': jax.random.normal(ks[4], (D, D), jnp.float32) * s, 'b_proj': jax.random.normal(ks[5], (D,), jnp.float32) * s, 'w_fc1': jax.random.normal(ks[6], (D, HID), jnp.float32) * s, 'b_fc1': jax.random.normal(ks[7], (HID,), jnp.float32) * s, 'w_fc2': jax.random.normal(ks[8], (HID, D), jnp.float32) * s, 'b_fc2': jax.random.normal(ks[9], (D,), jnp.float32) * s, 'w_ada': jax.random.normal(ks[10], (D, 6 * D), jnp.float32) * s, 'b_ada': jax.random.normal(ks[11], (6 * D,), jnp.float32) * s}
    _L1_cond_all = _L1_cond_setup()
    _L1_cond_in = {k: v for k, v in _L1_cond_all.items() if k in ('w_qkv', 'b_qkv', 'w_proj', 'b_proj', 'w_fc1', 'b_fc1', 'w_fc2', 'b_fc2', 'w_ada', 'b_ada')}
    del _L1_cond_all

    def _L2_cond_setup():
        import jax, jax.numpy as jnp
        import numpy as np
        B, L, C = (8, 128, 144)
        H = 16
        D = C // H
        FF = int(C * 4.0)
        EPS = 1e-06

        def _layernorm(x):
            mu = jnp.mean(x, axis=-1, keepdims=True)
            var = jnp.mean(jnp.square(x - mu), axis=-1, keepdims=True)
            return (x - mu) * jax.lax.rsqrt(var + EPS)

        def _modulate(x, shift, scale):
            return x * (1.0 + scale) + shift

        def _attention(h, W_qkv, b_qkv, W_proj, b_proj):
            b, l, c = h.shape
            qkv = h @ W_qkv + b_qkv
            qkv = qkv.reshape(b, l, 3, H, D)
            q, k, v = (qkv[:, :, 0], qkv[:, :, 1], qkv[:, :, 2])
            scale = D ** (-0.5)
            scores = jnp.einsum('blhd,bmhd->bhlm', q * scale, k)
            attn = jax.nn.softmax(scores, axis=-1)
            o = jnp.einsum('bhlm,bmhd->blhd', attn, v).reshape(b, l, c)
            return o @ W_proj + b_proj
        key = jax.random.key(seed)
        ks = jax.random.split(key, 12)
        s = 0.02
        return {'x': jax.random.normal(ks[0], (B, L, C), jnp.float32), 'c': jax.random.normal(ks[1], (B, 1, C), jnp.float32), 'W_qkv': jax.random.normal(ks[2], (C, 3 * C), jnp.float32) * s, 'b_qkv': jnp.zeros((3 * C,), jnp.float32), 'W_proj': jax.random.normal(ks[3], (C, C), jnp.float32) * s, 'b_proj': jnp.zeros((C,), jnp.float32), 'W_fc1': jax.random.normal(ks[4], (C, FF), jnp.float32) * s, 'b_fc1': jnp.zeros((FF,), jnp.float32), 'W_fc2': jax.random.normal(ks[5], (FF, C), jnp.float32) * s, 'b_fc2': jnp.zeros((C,), jnp.float32), 'W_ada': jax.random.normal(ks[6], (C, 6 * C), jnp.float32) * s, 'b_ada': jnp.zeros((6 * C,), jnp.float32)}
    _L2_cond_all = _L2_cond_setup()
    _L2_cond_in = {k: v for k, v in _L2_cond_all.items() if k in ('W_qkv', 'b_qkv', 'W_proj', 'b_proj', 'W_fc1', 'b_fc1', 'W_fc2', 'b_fc2', 'W_ada', 'b_ada')}
    del _L2_cond_all

    def _L3_cond_setup():
        import jax, jax.numpy as jnp
        import numpy as np
        B, S, D = (8, 128, 144)
        H = 16
        HD = D // H
        HID = int(D * 4.0)
        LN_EPS = 1e-05

        def layer_norm(x, w, b):
            m = jnp.mean(x, axis=-1, keepdims=True)
            v = jnp.mean(jnp.square(x - m), axis=-1, keepdims=True)
            return (x - m) * jax.lax.rsqrt(v + LN_EPS) * w + b

        def modulate(x, shift, scale):
            return x * (1.0 + scale[:, None, :]) + shift[:, None, :]

        def attention(x, wq, wk, wv, wo, wo_b):
            b, s, d = x.shape
            q = (x @ wq).reshape(b, s, H, HD).transpose(0, 2, 1, 3)
            k = (x @ wk).reshape(b, s, H, HD).transpose(0, 2, 1, 3)
            v = (x @ wv).reshape(b, s, H, HD).transpose(0, 2, 1, 3)
            scale = 1.0 / np.sqrt(HD).astype(np.float32)
            att = jnp.einsum('bhqd,bhkd->bhqk', q, k) * scale
            att = jax.nn.softmax(att, axis=-1)
            out = jnp.einsum('bhqk,bhkd->bhqd', att, v)
            out = out.transpose(0, 2, 1, 3).reshape(b, s, d)
            return out @ wo + wo_b
        key = jax.random.key(seed)
        ks = jax.random.split(key, 16)
        s = 0.02
        return {'x': jax.random.normal(ks[0], (B, S, D), jnp.float32), 'c': jax.random.normal(ks[1], (B, D), jnp.float32), 'ln1_w': jnp.ones((D,), jnp.float32), 'ln1_b': jnp.zeros((D,), jnp.float32), 'wq': jax.random.normal(ks[2], (D, D), jnp.float32) * s, 'wk': jax.random.normal(ks[3], (D, D), jnp.float32) * s, 'wv': jax.random.normal(ks[4], (D, D), jnp.float32) * s, 'wo': jax.random.normal(ks[5], (D, D), jnp.float32) * s, 'wo_b': jnp.zeros((D,), jnp.float32), 'ln2_w': jnp.ones((D,), jnp.float32), 'ln2_b': jnp.zeros((D,), jnp.float32), 'fc1_w': jax.random.normal(ks[6], (D, HID), jnp.float32) * s, 'fc1_b': jnp.zeros((HID,), jnp.float32), 'fc2_w': jax.random.normal(ks[7], (HID, D), jnp.float32) * s, 'fc2_b': jnp.zeros((D,), jnp.float32), 'ada_w': jax.random.normal(ks[8], (D, 6 * D), jnp.float32) * s, 'ada_b': jnp.zeros((6 * D,), jnp.float32)}
    _L3_cond_all = _L3_cond_setup()
    _L3_cond_in = {k: v for k, v in _L3_cond_all.items() if k in ('ln1_w', 'ln1_b', 'wq', 'wk', 'wv', 'wo', 'wo_b', 'ln2_w', 'ln2_b', 'fc1_w', 'fc1_b', 'fc2_w', 'fc2_b', 'ada_w', 'ada_b')}
    del _L3_cond_all
    return {'x': x, 'cond_1152': cond_1152, 'L0_cond_Wq': _L0_cond_in['Wq'], 'L0_cond_Wk': _L0_cond_in['Wk'], 'L0_cond_Wv': _L0_cond_in['Wv'], 'L0_cond_Wp': _L0_cond_in['Wp'], 'L0_cond_bp': _L0_cond_in['bp'], 'L0_cond_W1': _L0_cond_in['W1'], 'L0_cond_b1': _L0_cond_in['b1'], 'L0_cond_W2': _L0_cond_in['W2'], 'L0_cond_b2': _L0_cond_in['b2'], 'L0_cond_Wa': _L0_cond_in['Wa'], 'L0_cond_ba': _L0_cond_in['ba'], 'L1_cond_w_qkv': _L1_cond_in['w_qkv'], 'L1_cond_b_qkv': _L1_cond_in['b_qkv'], 'L1_cond_w_proj': _L1_cond_in['w_proj'], 'L1_cond_b_proj': _L1_cond_in['b_proj'], 'L1_cond_w_fc1': _L1_cond_in['w_fc1'], 'L1_cond_b_fc1': _L1_cond_in['b_fc1'], 'L1_cond_w_fc2': _L1_cond_in['w_fc2'], 'L1_cond_b_fc2': _L1_cond_in['b_fc2'], 'L1_cond_w_ada': _L1_cond_in['w_ada'], 'L1_cond_b_ada': _L1_cond_in['b_ada'], 'L2_cond_W_qkv': _L2_cond_in['W_qkv'], 'L2_cond_b_qkv': _L2_cond_in['b_qkv'], 'L2_cond_W_proj': _L2_cond_in['W_proj'], 'L2_cond_b_proj': _L2_cond_in['b_proj'], 'L2_cond_W_fc1': _L2_cond_in['W_fc1'], 'L2_cond_b_fc1': _L2_cond_in['b_fc1'], 'L2_cond_W_fc2': _L2_cond_in['W_fc2'], 'L2_cond_b_fc2': _L2_cond_in['b_fc2'], 'L2_cond_W_ada': _L2_cond_in['W_ada'], 'L2_cond_b_ada': _L2_cond_in['b_ada'], 'L3_cond_ln1_w': _L3_cond_in['ln1_w'], 'L3_cond_ln1_b': _L3_cond_in['ln1_b'], 'L3_cond_wq': _L3_cond_in['wq'], 'L3_cond_wk': _L3_cond_in['wk'], 'L3_cond_wv': _L3_cond_in['wv'], 'L3_cond_wo': _L3_cond_in['wo'], 'L3_cond_wo_b': _L3_cond_in['wo_b'], 'L3_cond_ln2_w': _L3_cond_in['ln2_w'], 'L3_cond_ln2_b': _L3_cond_in['ln2_b'], 'L3_cond_fc1_w': _L3_cond_in['fc1_w'], 'L3_cond_fc1_b': _L3_cond_in['fc1_b'], 'L3_cond_fc2_w': _L3_cond_in['fc2_w'], 'L3_cond_fc2_b': _L3_cond_in['fc2_b'], 'L3_cond_ada_w': _L3_cond_in['ada_w'], 'L3_cond_ada_b': _L3_cond_in['ada_b']}

def reference(x, cond_1152, L0_cond_Wq, L0_cond_Wk, L0_cond_Wv, L0_cond_Wp, L0_cond_bp, L0_cond_W1, L0_cond_b1, L0_cond_W2, L0_cond_b2, L0_cond_Wa, L0_cond_ba, L1_cond_w_qkv, L1_cond_b_qkv, L1_cond_w_proj, L1_cond_b_proj, L1_cond_w_fc1, L1_cond_b_fc1, L1_cond_w_fc2, L1_cond_b_fc2, L1_cond_w_ada, L1_cond_b_ada, L2_cond_W_qkv, L2_cond_b_qkv, L2_cond_W_proj, L2_cond_b_proj, L2_cond_W_fc1, L2_cond_b_fc1, L2_cond_W_fc2, L2_cond_b_fc2, L2_cond_W_ada, L2_cond_b_ada, L3_cond_ln1_w, L3_cond_ln1_b, L3_cond_wq, L3_cond_wk, L3_cond_wv, L3_cond_wo, L3_cond_wo_b, L3_cond_ln2_w, L3_cond_ln2_b, L3_cond_fc1_w, L3_cond_fc1_b, L3_cond_fc2_w, L3_cond_fc2_b, L3_cond_ada_w, L3_cond_ada_b):
    import jax
    import jax.numpy as jnp

    def _L0_cond_ref(x, c, Wq, Wk, Wv, Wp, bp, W1, b1, W2, b2, Wa, ba):
        import jax, jax.numpy as jnp
        import numpy as np
        B, T, D, H = (64, 32, 144, 16)
        HD = D // H
        EPS = 1e-06

        def _ln(x):
            mu = jnp.mean(x, axis=-1, keepdims=True)
            var = jnp.var(x, axis=-1, keepdims=True)
            return (x - mu) * jax.lax.rsqrt(var + EPS)

        def _modulate(x, shift, scale):
            return x * (1.0 + scale[:, None, :]) + shift[:, None, :]

        def _attn(x, Wq, Wk, Wv, Wp, bp):
            b, t, d = x.shape
            q = (x @ Wq).reshape(b, t, H, HD).transpose(0, 2, 1, 3)
            k = (x @ Wk).reshape(b, t, H, HD).transpose(0, 2, 1, 3)
            v = (x @ Wv).reshape(b, t, H, HD).transpose(0, 2, 1, 3)
            scores = jnp.einsum('bhqd,bhkd->bhqk', q, k) / np.sqrt(HD)
            mask = jnp.triu(jnp.ones((t, t), bool), k=1)
            scores = jnp.where(mask, -jnp.inf, scores)
            w = jax.nn.softmax(scores, axis=-1)
            ctx = jnp.einsum('bhqk,bhkd->bhqd', w, v).transpose(0, 2, 1, 3).reshape(b, t, d)
            return ctx @ Wp + bp

        def _mlp(x, W1, b1, W2, b2):
            return jax.nn.silu(x @ W1 + b1) @ W2 + b2
        mod = jax.nn.silu(c) @ Wa + ba
        sh_msa, sc_msa, g_msa, sh_mlp, sc_mlp, g_mlp = jnp.split(mod, 6, axis=1)
        x = x + g_msa[:, None, :] * _attn(_modulate(_ln(x), sh_msa, sc_msa), Wq, Wk, Wv, Wp, bp)
        x = x + g_mlp[:, None, :] * _mlp(_modulate(_ln(x), sh_mlp, sc_mlp), W1, b1, W2, b2)
        return x

    def _L1_cond_ref(x, t_emb, w_qkv, b_qkv, w_proj, b_proj, w_fc1, b_fc1, w_fc2, b_fc2, w_ada, b_ada):
        import jax, jax.numpy as jnp
        import numpy as np
        B, N, D = (8, 128, 144)
        H = 16
        HD = D // H
        HID = 4 * D
        EPS = 1e-06

        def _ln(x):
            mu = jnp.mean(x, axis=-1, keepdims=True)
            var = jnp.mean(jnp.square(x - mu), axis=-1, keepdims=True)
            return (x - mu) * jax.lax.rsqrt(var + EPS)

        def _modulate(x, shift, scale):
            return x * (1.0 + scale[:, None, :]) + shift[:, None, :]

        def _attn(x, w_qkv, b_qkv, w_proj, b_proj):
            b, n, d = x.shape
            qkv = (x @ w_qkv + b_qkv).reshape(b, n, 3, H, HD)
            q = qkv[:, :, 0].transpose(0, 2, 1, 3)
            k = qkv[:, :, 1].transpose(0, 2, 1, 3)
            v = qkv[:, :, 2].transpose(0, 2, 1, 3)
            scores = jnp.einsum('bhnd,bhmd->bhnm', q, k) * HD ** (-0.5)
            attn = jax.nn.softmax(scores, axis=-1)
            out = jnp.einsum('bhnm,bhmd->bhnd', attn, v)
            out = out.transpose(0, 2, 1, 3).reshape(b, n, d)
            return out @ w_proj + b_proj
        ada = jax.nn.silu(t_emb) @ w_ada + b_ada
        shift_a, scale_a, gate_a, shift_f, scale_f, gate_f = jnp.split(ada, 6, axis=-1)
        x = x + gate_a[:, None, :] * _attn(_modulate(_ln(x), shift_a, scale_a), w_qkv, b_qkv, w_proj, b_proj)
        h = _modulate(_ln(x), shift_f, scale_f)
        h = jax.nn.gelu(h @ w_fc1 + b_fc1, approximate=True) @ w_fc2 + b_fc2
        return x + gate_f[:, None, :] * h

    def _L2_cond_ref(x, c, W_qkv, b_qkv, W_proj, b_proj, W_fc1, b_fc1, W_fc2, b_fc2, W_ada, b_ada):
        import jax, jax.numpy as jnp
        import numpy as np
        B, L, C = (8, 128, 144)
        H = 16
        D = C // H
        FF = int(C * 4.0)
        EPS = 1e-06

        def _layernorm(x):
            mu = jnp.mean(x, axis=-1, keepdims=True)
            var = jnp.mean(jnp.square(x - mu), axis=-1, keepdims=True)
            return (x - mu) * jax.lax.rsqrt(var + EPS)

        def _modulate(x, shift, scale):
            return x * (1.0 + scale) + shift

        def _attention(h, W_qkv, b_qkv, W_proj, b_proj):
            b, l, c = h.shape
            qkv = h @ W_qkv + b_qkv
            qkv = qkv.reshape(b, l, 3, H, D)
            q, k, v = (qkv[:, :, 0], qkv[:, :, 1], qkv[:, :, 2])
            scale = D ** (-0.5)
            scores = jnp.einsum('blhd,bmhd->bhlm', q * scale, k)
            attn = jax.nn.softmax(scores, axis=-1)
            o = jnp.einsum('bhlm,bmhd->blhd', attn, v).reshape(b, l, c)
            return o @ W_proj + b_proj
        ada = jax.nn.silu(c) @ W_ada + b_ada
        shift_msa, scale_msa, gate_msa, shift_mlp, scale_mlp, gate_mlp = jnp.split(ada, 6, axis=-1)
        h = _modulate(_layernorm(x), shift_msa, scale_msa)
        x = x + gate_msa * _attention(h, W_qkv, b_qkv, W_proj, b_proj)
        h = _modulate(_layernorm(x), shift_mlp, scale_mlp)
        mlp = jax.nn.gelu(h @ W_fc1 + b_fc1, approximate=True) @ W_fc2 + b_fc2
        x = x + gate_mlp * mlp
        return x

    def _L3_cond_ref(x, c, ln1_w, ln1_b, wq, wk, wv, wo, wo_b, ln2_w, ln2_b, fc1_w, fc1_b, fc2_w, fc2_b, ada_w, ada_b):
        import jax, jax.numpy as jnp
        import numpy as np
        B, S, D = (8, 128, 144)
        H = 16
        HD = D // H
        HID = int(D * 4.0)
        LN_EPS = 1e-05

        def layer_norm(x, w, b):
            m = jnp.mean(x, axis=-1, keepdims=True)
            v = jnp.mean(jnp.square(x - m), axis=-1, keepdims=True)
            return (x - m) * jax.lax.rsqrt(v + LN_EPS) * w + b

        def modulate(x, shift, scale):
            return x * (1.0 + scale[:, None, :]) + shift[:, None, :]

        def attention(x, wq, wk, wv, wo, wo_b):
            b, s, d = x.shape
            q = (x @ wq).reshape(b, s, H, HD).transpose(0, 2, 1, 3)
            k = (x @ wk).reshape(b, s, H, HD).transpose(0, 2, 1, 3)
            v = (x @ wv).reshape(b, s, H, HD).transpose(0, 2, 1, 3)
            scale = 1.0 / np.sqrt(HD).astype(np.float32)
            att = jnp.einsum('bhqd,bhkd->bhqk', q, k) * scale
            att = jax.nn.softmax(att, axis=-1)
            out = jnp.einsum('bhqk,bhkd->bhqd', att, v)
            out = out.transpose(0, 2, 1, 3).reshape(b, s, d)
            return out @ wo + wo_b
        mod = jax.nn.silu(c) @ ada_w + ada_b
        sh_msa, sc_msa, g_msa, sh_mlp, sc_mlp, g_mlp = jnp.split(mod, 6, axis=1)
        h = modulate(layer_norm(x, ln1_w, ln1_b), sh_msa, sc_msa)
        x = x + g_msa[:, None, :] * attention(h, wq, wk, wv, wo, wo_b)
        h = modulate(layer_norm(x, ln2_w, ln2_b), sh_mlp, sc_mlp)
        h = jax.nn.gelu(h @ fc1_w + fc1_b, approximate=False) @ fc2_w + fc2_b
        x = x + g_mlp[:, None, :] * h
        return x
    x = _L0_cond_ref(x, cond_1152, L0_cond_Wq, L0_cond_Wk, L0_cond_Wv, L0_cond_Wp, L0_cond_bp, L0_cond_W1, L0_cond_b1, L0_cond_W2, L0_cond_b2, L0_cond_Wa, L0_cond_ba)
    x = _L1_cond_ref(x, cond_1152, L1_cond_w_qkv, L1_cond_b_qkv, L1_cond_w_proj, L1_cond_b_proj, L1_cond_w_fc1, L1_cond_b_fc1, L1_cond_w_fc2, L1_cond_b_fc2, L1_cond_w_ada, L1_cond_b_ada)
    x = _L2_cond_ref(x, cond_1152[:, None, :], L2_cond_W_qkv, L2_cond_b_qkv, L2_cond_W_proj, L2_cond_b_proj, L2_cond_W_fc1, L2_cond_b_fc1, L2_cond_W_fc2, L2_cond_b_fc2, L2_cond_W_ada, L2_cond_b_ada)
    x = _L3_cond_ref(x, cond_1152, L3_cond_ln1_w, L3_cond_ln1_b, L3_cond_wq, L3_cond_wk, L3_cond_wv, L3_cond_wo, L3_cond_wo_b, L3_cond_ln2_w, L3_cond_ln2_b, L3_cond_fc1_w, L3_cond_fc1_b, L3_cond_fc2_w, L3_cond_fc2_b, L3_cond_ada_w, L3_cond_ada_b)
    return x

_drawn_inputs = setup_inputs


def setup_inputs(seed=0):
    import zlib

    import numpy as np

    out = dict(_drawn_inputs(seed))
    spreads = {'L0_cond_bp': (0.0, 0.1),
     'L0_cond_b1': (0.0, 0.1),
     'L0_cond_b2': (0.0, 0.1),
     'L0_cond_ba': (0.0, 0.1),
     'L2_cond_b_qkv': (0.0, 0.8),
     'L2_cond_b_proj': (0.0, 0.515),
     'L2_cond_b_fc1': (0.0, 0.8),
     'L2_cond_b_fc2': (0.0, 0.569),
     'L2_cond_b_ada': (0.0, 0.572),
     'L3_cond_ln1_w': (1.0, 0.6),
     'L3_cond_ln1_b': (0.0, 0.8),
     'L3_cond_wo_b': (0.0, 0.596),
     'L3_cond_ln2_w': (1.0, 0.6),
     'L3_cond_ln2_b': (0.0, 0.8),
     'L3_cond_fc1_b': (0.0, 0.8),
     'L3_cond_fc2_b': (0.0, 1.475),
     'L3_cond_ada_b': (0.0, 0.65)}
    factors = {'L1_cond_w_qkv': 8.0,
     'L1_cond_b_qkv': 8.0,
     'L1_cond_w_proj': 8.0,
     'L1_cond_b_proj': 8.0,
     'L1_cond_w_fc1': 8.0,
     'L1_cond_b_fc1': 8.0,
     'L1_cond_w_fc2': 8.0,
     'L1_cond_b_fc2': 31.531,
     'L1_cond_w_ada': 6.377,
     'L1_cond_b_ada': 8.0,
     'L2_cond_W_qkv': 8.0,
     'L2_cond_W_proj': 8.0,
     'L2_cond_W_fc1': 6.172,
     'L2_cond_W_fc2': 5.74,
     'L2_cond_W_ada': 2.99,
     'L3_cond_wq': 8.0,
     'L3_cond_wk': 8.0,
     'L3_cond_wv': 8.0,
     'L3_cond_wo': 8.0,
     'L3_cond_fc1_w': 5.938,
     'L3_cond_fc2_w': 5.417,
     'L3_cond_ada_w': 2.839}
    for name, (base, spread) in spreads.items():
        noise = np.random.default_rng([zlib.crc32(name.encode()), seed]).standard_normal(out[name].shape)
        drawn = base * np.exp(spread * noise) if base else spread * noise
        out[name] = jnp.asarray(drawn.astype(out[name].dtype))
    for name, factor in factors.items():
        out[name] = (out[name] * factor).astype(out[name].dtype)
    return out
```

```python
from contextlib import ExitStack

import concourse.bass as bass
from concourse import mybir

F32 = mybir.dt.float32
F32R = mybir.dt.float32r
BF16 = mybir.dt.bfloat16
ACT = mybir.ActivationFunctionType
ALU = mybir.AluOpType
AX_X = mybir.AxisListType.X

P = 128
LAYERS = 4
B, T, D = 2, 512, 144
HEADS = 16
HD = D // HEADS
HID = 4 * D
TT = T // P
QUAD = 4
GROUPS = HEADS // QUAD
DREM = D - P
REM = 3 * DREM + 2
SROWS = 3 * HD
MROW = SROWS
PADD = 32
SUM = 2 * HD
HT = -(-HID // P)
HLAST = HID - (HT - 1) * P
LEAD = 5
UNITS = [(l, b, g) for l in range(LAYERS) for b in range(B) for g in range(GROUPS)]
QUARTERS = TT * len(UNITS)
EPS = (1e-6, 1e-6, 1e-6, 1e-5)
MLP_FUNC = (ACT.Silu, ACT.Gelu_apprx_tanh, ACT.Gelu_apprx_tanh, ACT.Gelu)
NEG = -1e30
NC = 8
SCALE = HD ** -0.5


class Step:

    def __init__(self, kind, a, bj, n, l=0, b=0, half=0, side=0, gp=0, gg=0, p=0, u=0, t=0, e=None, m=None):
        self.kind, self.a, self.bj, self.n = kind, a, bj, n
        self.l, self.b, self.half = l, b, half
        self.side, self.gp, self.gg, self.p = side, gp, gg, p
        self.u, self.t, self.e, self.m = u, t, e, m


def make_plan():
    plan = []
    jobs = {"a": 0, "b": 0}
    made = {}

    def add(kind, a=0, bb=0, **k):
        plan.append(Step(kind, jobs["a"], jobs["b"], made.get(kind, 0), **k))
        jobs["a"] += a
        jobs["b"] += bb
        made[kind] = made.get(kind, 0) + 1

    def chain(l, b):
        at = {0: [("copy", dict(b=b, gg=1)), ("norm", dict(b=b, gg=1, p=0)), ("norm", dict(b=b, gg=1, p=1))],
              1: [("norm", dict(b=b, gg=1, p=2)), ("norm", dict(b=b, gg=1, p=3))],
              2: [("proj", dict(a=1, l=l, b=b))],
              4: [("spread", dict(bb=2, l=l, b=b, half=1))],
              5: [("w1", dict(bb=HT, l=l, b=b))],
              6: [("w2", dict(a=1, l=l, b=b))]}
        if l + 1 < LAYERS:
            at.update(entry(l + 1, b))
        return at

    def entry(l, b):
        return {8: [("spread", dict(bb=2, l=l, b=b, half=0))],
                9: [("qk", dict(a=1, l=l, b=b, side=1, gp=0))],
                10: [("qk", dict(a=1, l=l, b=b, side=0, gp=0))],
                11: [("v", dict(bb=2, l=l, b=b)), ("qk", dict(a=1, l=l, b=b, side=1, gp=1))],
                12: [("qk", dict(a=1, l=l, b=b, side=0, gp=1))]}

    add("stats", b=0)
    for steps in entry(0, 0).values():
        for kind, k in steps:
            add(kind, **k)
    dense = {2: [("stats", dict(b=1))]}
    for k, v in entry(0, 1).items():
        dense.setdefault(k - 4, []).extend(v)
    for l in range(LAYERS):
        for b in range(B):
            own = 4 * GROUPS * (B * l + b)
            dense.setdefault(own + 8, []).extend(
                [("copy", dict(b=b, gg=0)), ("norm", dict(b=b, gg=0, p=0))])
            for p in (1, 2, 3):
                dense.setdefault(own + 8 + p, []).append(("norm", dict(b=b, gg=0, p=p)))
            for k, v in chain(l, b).items():
                dense.setdefault(own + 16 + k, []).extend(v)
    for t in range(-LEAD, max(max(dense) + 1, QUARTERS + 1)):
        if t >= -1 and t % TT == TT - 1 and t < QUARTERS - 1:
            add("shift", a=1, u=(t + 1) // TT)
        e = t if 0 <= t < QUARTERS else None
        m = t + LEAD if t + LEAD < QUARTERS else None
        if e is not None or m is not None or t == QUARTERS:
            add("attend", a=0 if m is None else 2, bb=0 if e is None else QUAD, t=t, e=e, m=m)
        for kind, k in dense.get(t, []):
            add(kind, **k)
    return plan


def span(l, tile):
    return P * tile if l == 0 else 0


def program(nc, A, out):
    plan = make_plan()
    ctx = ExitStack()
    with ctx:
        def sb(name, shape, dt=F32):
            return ctx.enter_context(nc.sbuf_tensor(name, shape, dt))

        def sem(name):
            return ctx.enter_context(nc.semaphore(name))

        X = sb("X", [P, B * TT, D])
        w_qk = sb("w_qk", [P, 2, 2, GROUPS, P])
        r_qk = sb("r_qk", [REM, 2, 2, GROUPS, P], F32R)
        raw_qk = sb("raw_qk", [P, 2 * D])
        w_v = sb("w_v", [P, LAYERS, D])
        w_1 = sb("w_1", [P, LAYERS, HID])
        NR = 3 * D + HID
        raw_r = sb("raw_r", [REM, NR])
        r_mu = sb("r_mu", [REM, NR])
        r_vw = sb("r_vw", [REM, LAYERS, D + HID], F32R)
        w_2 = sb("w_2", [P, LAYERS, HT, D])
        w_p = sb("w_p", [P, LAYERS, 2, D])
        cT = sb("cT", [P, B])
        cR = sb("cR", [P, B])
        sT = sb("sT", [P, B])
        sR = sb("sR", [P, B])
        sTb = sb("sTb", [P, B, P])
        sRb = sb("sRb", [P, B, P])
        mod = sb("mod", [P, LAYERS, 4, B])
        modr = sb("modr", [REM, LAYERS, 4, B])
        lnw = sb("lnw", [P, 4])
        lnwr = sb("lnwr", [REM, 4])
        gate = sb("gate", [P, LAYERS, 2, B, D])
        consts = sb("consts", [P, NC])
        kones = sb("kones", [REM, PADD - SROWS])
        ident = sb("ident", [P, P])
        identb = sb("identb", [P, P], BF16)
        maskS = sb("maskS", [P, P], BF16)
        maskT = sb("maskT", [P, P], BF16)
        half = sb("half", [P, TT])
        Qs = sb("Qs", [P, B, GROUPS, T], F32R)
        Ks = sb("Ks", [P, B, GROUPS, T], F32R)
        V = sb("V", [P, B, TT, HEADS, PADD])
        probs = sb("probs", [P, 2 * QUAD, T])
        ada = probs[:, :, :].rearrange("p a b -> p (a b)")[:, 0:LAYERS * 6 * D].rearrange(
            "p (l n) -> p l n", l=LAYERS)
        part = sb("part", [P, 2, T], F32R)
        mx = sb("mx", [P, TT, QUAD])
        mrow = sb("mrow", [P, TT, P], BF16)
        ctxS = sb("ctxS", [P, T])
        ctxN = sb("ctxN", [P, 2, T])
        adar = ctxN[:, :, :].rearrange("p a b -> p (a b)")[:, 0:6 * D]
        sums = sb("sums", [P, P])
        rsum = sb("rsum", [P, P])
        tmp = sb("tmp", [P, TT, D])
        st = sb("st", [P, TT, 6])
        mv = sb("mv", [P, TT, 2])
        ve = sb("ve", [P, TT])
        rstd = sb("rstd", [P, TT])
        XE = 180
        xe = sb("xe", [P, TT, XE])
        hmain = sb("hmain", [P, T])
        yrem = sb("yrem", [REM, T])
        hrnd = sb("hrnd", [REM, T])
        hrem = sb("hrem", [REM, T], F32R)
        hid = sb("hid", [P, HT, T])
        N3 = 4 * 3 * DREM
        hid_flat = hid[:, :, :].rearrange("p a b -> p (a b)")
        ada3 = hid_flat[:, 0:LAYERS * N3].rearrange("p (l n) -> p l n", l=LAYERS)
        adar3 = hid_flat[:, LAYERS * N3:(LAYERS + 1) * N3]

        ringA = ctx.enter_context(nc.psum_tensor("ringA", [P, 2, 2, T], F32))
        ringB = ctx.enter_context(nc.psum_tensor("ringB", [P, 3, T], F32))
        ctxP = ctx.enter_context(nc.psum_tensor("ctxP", [P, T], F32))

        def gate_out(l, h, b):
            bank, at = divmod((l * 2 + h) * B + b, 3)
            where = (ringA[:, 1, 0, :], ringA[:, 1, 1, :], ringB[:, 0, :], ringB[:, 1, :], ringB[:, 2, :],
                     ctxP[:, :])[bank]
            return where[:, at * D:(at + 1) * D]

        small_in = sem("small_in")
        x_in = sem("x_in")
        w_in = [sem(f"w_in{l}") for l in range(LAYERS)]
        ada_in = sem("ada_in")
        cleared = sem("cleared")
        consts_ok = sem("consts_ok")
        pool_ops = sem("pool_ops")
        dve_ops = sem("dve_ops")
        silu_c = sem("silu_c")
        silu_b = sem("silu_b")
        mod_mm = sem("mod_mm")
        mod_read = sem("mod_read")
        mod_ok = sem("mod_ok")
        w_ok = sem("w_ok")
        a_ready, a_free = sem("a_ready"), sem("a_free")
        b_ready, b_free = sem("b_ready"), sem("b_free")
        rounded = sem("rounded")
        mrow_ok = sem("mrow_ok")
        pv_done = sem("pv_done")
        ctx_free = sem("ctx_free")
        norm_ok = sem("norm_ok")
        stats_ok = sem("stats_ok")
        xhat_ok = sem("xhat_ok")
        hrem_ok = sem("hrem_ok")
        x_done = sem("x_done")
        stored = sem("stored")

        exps_before = {}
        for s in plan:
            if s.kind == "attend" and s.e is not None:
                exps_before[s.e] = s.bj + QUAD
        shift_job = {s.u: s.a for s in plan if s.kind == "shift"}
        qk_job = {(s.l, s.b, s.side, s.gp): s for s in plan if s.kind == "qk"}
        v_job = {(s.l, s.b): s for s in plan if s.kind == "v"}
        ln_job = {(s.l, s.b, s.half): s for s in plan if s.kind == "spread"}
        w1_job = {(s.l, s.b): s for s in plan if s.kind == "w1"}
        qk_steps = [s for s in plan if s.kind == "qk"]
        ln_steps = [s for s in plan if s.kind == "spread"]

        n_w = [0] * LAYERS
        n_small = [0]
        block = ctx.enter_context(nc.Block())

        def load(eng, semaphore, dst, src, counter, i=0):
            eng.dma_start(dst, src).then_inc(semaphore, 16)
            counter[i] += 16

        n_ada = [0]

        def load_layer(eng, l):
            if l > 0:
                eng.wait_ge(w_ok, l)
            load(eng, w_in[l], raw_qk[:, :], A["w_main"][l, :, 0:2 * D], n_w, l)
            load(eng, w_in[l], raw_r[:, :], A["w_rem"][l], n_w, l)
            load(eng, w_in[l], w_v[:, l, :], A["w_main"][l, :, 2 * D:3 * D], n_w, l)
            load(eng, w_in[l], w_1[:, l, :], A["w_main"][l, :, 3 * D:NR], n_w, l)
            load(eng, w_in[l], w_p[:, l, :, :], A["w_p"][l], n_w, l)
            load(eng, w_in[l], w_2[:, l, :, :], A["w_2"][l], n_w, l)

        @block.sync
        def _(sp):
            x_v = A["x"].rearrange("b (t p) d -> p (b t) d", p=P)
            sp.dma_start(X[:, :, :], x_v).then_inc(x_in, 16)
            load_layer(sp, 0)
            load(sp, ada_in, ada, A["ada_main"], n_ada)
            load(sp, ada_in, adar, A["ada_rem"], n_ada)
            load(sp, ada_in, ada3, A["ada3_main"], n_ada)
            load(sp, ada_in, adar3, A["ada3_rem"], n_ada)
            for l in range(1, LAYERS):
                load_layer(sp, l)
            out_v = out.rearrange("b (t p) d -> p (b t) d", p=P)
            for b in range(B):
                sp.wait_ge(x_done, b + 1)
                sp.dma_start(out_v[:, b * TT:(b + 1) * TT, :], X[:, b * TT:(b + 1) * TT, :]).then_inc(stored, 16)
            sp.wait_ge(stored, 16 * B)

        @block.scalar
        def _(act):
            load(act, small_in, cT[:, :], A["c_main"], n_small)
            load(act, small_in, cR[:, :], A["c_rem"], n_small)
            load(act, small_in, consts[:, :], A["consts"], n_small)
            load(act, small_in, kones[:, :], A["kones"], n_small)
            load(act, small_in, lnw[:, :], A["ln_main"], n_small)
            load(act, small_in, lnwr[:, :], A["ln_rem"], n_small)
            load(act, small_in, modr[3 * DREM:REM, :, :, :].rearrange("p a b c -> p (a b c)"),
                 A["modones"], n_small)
            act.wait_ge(small_in, n_small[0])
            nc.scalar.activation(sT[:, :], cT[:, :], ACT.Silu).then_inc(silu_c, 1)
            nc.scalar.activation(sR[:, :], cR[:, :], ACT.Silu).then_inc(silu_c, 1)

            for s in plan:
                if s.kind == "attend" and s.e is not None:
                    l, b, g = UNITS[s.e // TT]
                    kt = s.e % TT
                    q0 = span(l, kt)
                    base = min(q0, T - 2 * P)
                    for j in range(QUAD):
                        job = s.bj + j
                        act.wait_ge(b_ready, job + 1)
                        if s.e >= 2:
                            act.wait_ge(pv_done, s.e - 1)
                        nc.scalar.activation(probs[:, QUAD * (s.e % 2) + j, q0:T],
                                             ringB[:, job % 3, q0 - base:T - base],
                                             ACT.Exp, scale=SCALE).then_inc(b_free, 1)
                elif s.kind == "spread":
                    v0 = 2 * s.half
                    if s.n == 0:
                        act.wait_ge(mod_ok, 1)
                    act.wait_ge(b_ready, s.bj + 1)
                    nc.scalar.activation(hmain[:, :], ringB[:, s.bj % 3, :], ACT.Identity,
                                         scale=mod[:, s.l, v0 + 1, s.b:s.b + 1],
                                         bias=mod[:, s.l, v0, s.b:s.b + 1]).then_inc(b_free, 1)
                    act.wait_ge(b_ready, s.bj + 2)
                    if s.n >= 1:
                        act.wait_ge(hrem_ok, s.n)
                    nc.scalar.activation(yrem[:, :], ringB[0:REM, (s.bj + 1) % 3, :], ACT.Identity,
                                         scale=modr[:, s.l, v0 + 1, s.b:s.b + 1],
                                         bias=modr[:, s.l, v0, s.b:s.b + 1]).then_inc(b_free, 1)
                elif s.kind == "qk":
                    act.wait_ge(a_ready, s.a + 1)
                    if s.n >= 1:
                        act.wait_ge(a_free, qk_steps[s.n - 1].a + 1)
                    nc.scalar.activation(part[:, :, :], ringA[:, s.a % 2, :, :], ACT.Copy).then_inc(rounded, 1)
                elif s.kind == "v":
                    for i in range(2):
                        job = s.bj + i
                        act.wait_ge(b_ready, job + 1)
                        if s.n == 0 and i == 0:
                            act.wait_ge(cleared, 1)
                        for k in range(2):
                            tt = 2 * i + k
                            for gg in range(2):
                                src = ringB[:, job % 3, k * D + gg * 8 * HD:k * D + (gg + 1) * 8 * HD].rearrange(
                                    "p (s j d) -> p s j d", s=2, j=QUAD)
                                for sx in range(2):
                                    h0 = 8 * gg + QUAD * sx
                                    last = nc.scalar.activation(V[:, s.b, tt, h0:h0 + QUAD, HD * sx:HD * sx + HD],
                                                                src[:, sx], ACT.Copy)
                        last.then_inc(b_free, 1)
                elif s.kind == "w1":
                    for m in range(HT):
                        rows = P if m < HT - 1 else HLAST
                        act.wait_ge(b_ready, s.bj + m + 1)
                        nc.scalar.activation(hid[0:rows, m, :], ringB[0:rows, (s.bj + m) % 3, :],
                                             MLP_FUNC[s.l]).then_inc(b_free, 1)

        @block.gpsimd
        def _(pool):
            done = [0]

            def then(ins):
                done[0] += 1
                return ins.then_inc(pool_ops, 1)

            def settled():
                pool.wait_ge(pool_ops, done[0])

            then(nc.gpsimd.memset(half[:, :], -0.5))
            then(nc.gpsimd.memset(xe[:, :, D + 2 * DREM:XE], 0.0))
            for m in (ident, identb, maskS, maskT):
                then(nc.gpsimd.memset(m[:, :], 0.0))
            settled()
            for m in (ident, identb):
                then(nc.gpsimd.affine_select(out=m[:, :], in_=m[:, :], compare_op=ALU.not_equal, fill=1.0,
                                             base=0, pattern=[[-1, P]], channel_multiplier=1))
            then(nc.gpsimd.affine_select(out=maskS[:, :], in_=maskS[:, :], compare_op=ALU.is_ge, fill=NEG,
                                         base=0, pattern=[[-1, P]], channel_multiplier=1))
            then(nc.gpsimd.affine_select(out=maskT[:, :], in_=maskT[:, :], compare_op=ALU.is_ge, fill=NEG,
                                         base=0, pattern=[[1, P]], channel_multiplier=-1))
            settled()
            nc.gpsimd.memset(hid[HLAST:HLAST + 1, HT - 1, :], 1.0).then_inc(consts_ok, 1)
            pool.wait_ge(consts_ok, 1)
            then(nc.gpsimd.memset(V[:, :, :, :, HD:PADD], 0.0))
            then(nc.gpsimd.memset(V[:, :, :, :, 0:HD], 0.0))
            settled()
            for b in range(B):
                for sx in range(2):
                    v = V[:, b, :, :, SUM + sx:SUM + sx + 1].rearrange("p t (g s j) c -> p s (t g) (j c)", g=2, s=2)
                    then(nc.gpsimd.memset(v[:, sx], 1.0))
            settled()
            nc.gpsimd.memset(mrow[:, :, :], 0.0).then_inc(cleared, 1)

            def stack_weights(l):
                pool.wait_ge(w_in[l], n_w[l])
                if l == 0:
                    pool.wait_ge(small_in, n_small[0])
                if l >= 2:
                    pool.wait_ge(a_ready, qk_job[l - 2, B - 1, 0, 1].a + 1)
                settled()
                then(nc.gpsimd.tensor_copy(r_mu[:, :].bitcast(F32R), raw_r[:, :]))
                settled()
                then(nc.gpsimd.tensor_scalar(r_mu[:, :], r_mu[:, :], consts[0:REM, 3:4], None, ALU.mult))
                settled()
                then(nc.gpsimd.tensor_tensor(r_vw[:, l, :], raw_r[:, 2 * D:NR], r_mu[:, 2 * D:NR], ALU.add))
                then(nc.gpsimd.tensor_tensor(raw_r[:, 0:2 * D], raw_r[:, 0:2 * D], r_mu[:, 0:2 * D], ALU.add))
                settled()
                for i in range(2):
                    for dst, raw in ((w_qk, raw_qk), (r_qk, raw_r)):
                        to = dst[:, l % 2, i].rearrange("p g (j c) -> p (g j) c", c=PADD)
                        frm = raw[:, i * D:(i + 1) * D].rearrange("p (h d) -> p h d", d=HD)
                        for r in range(3):
                            then(nc.gpsimd.tensor_copy(to[:, :, r * HD:(r + 1) * HD], frm))
                        pad = to[:, :, SROWS:PADD]
                        if dst is r_qk and i == 1:
                            ones = kones[:, :].rearrange("p (a c) -> p a c", a=1).broadcast_to(
                                [REM, HEADS, PADD - SROWS])
                            then(nc.gpsimd.tensor_copy(pad, ones))
                        elif dst is r_qk:
                            then(nc.gpsimd.memset(pad.bitcast(F32), 0.0))
                        else:
                            then(nc.gpsimd.memset(pad, 0.0))
                settled()
                nc.gpsimd.tensor_copy(half[:, 0:1], half[:, 1:2]).then_inc(w_ok, 1)

            stack_weights(0)
            for s in plan:
                if s.kind == "spread":
                    pool.wait_ge(stats_ok, s.n + 1)
                    settled()
                    then(nc.gpsimd.tensor_scalar(ve[:, :], mv[:, :, 1], EPS[s.l], None, ALU.add))
                    settled()
                    then(nc.gpsimd.tensor_tensor(rstd[:, :], ve[:, :], half[:, :], ALU.pow))
                    settled()
                    if s.n >= 1:
                        pool.wait_ge(b_ready, ln_steps[s.n - 1].bj + 2)
                    for tt in range(TT):
                        x = X[:, s.b * TT + tt, :]
                        then(nc.gpsimd.tensor_scalar(xe[:, tt, 0:P], x[:, 0:P], mv[:, tt, 0:1],
                                                     rstd[:, tt:tt + 1], ALU.subtract, ALU.mult))
                        rep = x[:, P:D].rearrange("p (a c) -> p a c", a=1).broadcast_to([P, 3, DREM])
                        then(nc.gpsimd.tensor_scalar(
                            xe[:, tt, P:P + 3 * DREM].rearrange("p (a c) -> p a c", a=3), rep,
                            mv[:, tt, 0:1], rstd[:, tt:tt + 1], ALU.subtract, ALU.mult))
                    settled()
                    nc.gpsimd.tensor_copy(ve[:, 0:1], ve[:, 1:2]).then_inc(xhat_ok, 1)
                    pool.wait_ge(b_free, s.bj + 2)
                    then(nc.gpsimd.tensor_copy(hrnd[:, :].bitcast(F32R), yrem[:, :]))
                    settled()
                    then(nc.gpsimd.tensor_scalar(hrnd[:, :], hrnd[:, :], consts[0:REM, 2:3], None, ALU.mult))
                    settled()
                    nc.gpsimd.tensor_tensor(hrem[:, :], yrem[:, :], hrnd[:, :], ALU.add).then_inc(hrem_ok, 1)
                    if s.n == 0:
                        stack_weights(1)
                    elif s.b == B - 1 and s.half == 1 and s.l < LAYERS - 2:
                        stack_weights(s.l + 2)

        @block.vector
        def _(dve):
            done = [0]

            def then(ins):
                done[0] += 1
                return ins.then_inc(dve_ops, 1)

            def settled():
                dve.wait_ge(dve_ops, done[0])

            dve.wait_ge(silu_c, 2)
            dve.wait_ge(small_in, n_small[0])
            then(nc.vector.tensor_scalar(sR[:, :], sR[:, :], consts[:, 4:5], consts[:, 5:6], ALU.mult, ALU.add))
            settled()
            then(nc.vector.tensor_copy(sTb[:, :, :], sT[:, :].rearrange("p (b a) -> p b a", a=1).broadcast_to([P, B, P])))
            nc.vector.tensor_copy(sRb[:, :, :], sR[:, :].rearrange("p (b a) -> p b a", a=1).broadcast_to(
                [P, B, P])).then_inc(silu_b, 1)
            settled()
            dve.wait_ge(silu_b, 1)
            dve.wait_ge(mod_mm, LAYERS)
            src = ringA[:, 0, 0, 0:LAYERS * 4 * B].rearrange("p (l v b) -> p l v b", l=LAYERS, v=4)
            srcr = ringA[0:3 * DREM, 0, 1, 0:LAYERS * 4 * B].rearrange("p (l v b) -> p l v b", l=LAYERS, v=4)
            modc = modr[0:3 * DREM]
            for dst, frm in ((mod, src), (modc, srcr)):
                for h in range(2):
                    then(nc.vector.tensor_copy(dst[:, :, 2 * h, :], frm[:, :, 2 * h, :]))
                    then(nc.vector.tensor_scalar(dst[:, :, 2 * h + 1, :], frm[:, :, 2 * h + 1, :], 1.0, None, ALU.add))
            settled()
            for dst, wb in ((mod, lnw), (modc, lnwr[0:3 * DREM])):
                for h in range(2):
                    sh, sc = dst[:, LAYERS - 1, 2 * h, :], dst[:, LAYERS - 1, 2 * h + 1, :]
                    then(nc.vector.scalar_tensor_tensor(out=sh, in0=sc, scalar=wb[:, 2 * h:2 * h + 1], in1=sh,
                                                        op0=ALU.mult, op1=ALU.add))
                    settled()
                    then(nc.vector.tensor_scalar(sc, sc, wb[:, 2 * h + 1:2 * h + 2], None, ALU.mult))
            settled()
            nc.vector.memset(ctxS[:, 0:2], 0.0).then_inc(mod_ok, 1)
            for l in range(LAYERS):
                for h in range(2):
                    for b in range(B):
                        cp = nc.vector.tensor_copy(gate[:, l, h, b, :], gate_out(l, h, b))
                        if (l, h, b) == (LAYERS - 1, 1, B - 1):
                            cp.then_inc(mod_ok, 1)
                        else:
                            then(cp)
            dve.wait_ge(mod_ok, 2)
            settled()

            stats_made = [0]

            def stats(b):
                if stats_made[0]:
                    dve.wait_ge(xhat_ok, stats_made[0])
                stats_made[0] += 1
                for tt in range(TT):
                    then(nc.vector.bn_stats(st[:, tt, :], X[:, b * TT + tt, :]))
                settled()
                for tt in range(TT):
                    cp = nc.vector.bn_aggr(mv[:, tt, :], st[:, tt, :])
                    if tt == TT - 1:
                        cp.then_inc(stats_ok, 1)
                    else:
                        then(cp)

            def residual(s, h, last_use):
                dve.wait_ge(a_ready, s.a + 1)
                prod = ringA[:, s.a % 2, :, 0:2 * D]
                for k in range(2):
                    g = gate[:, s.l, h, s.b, :].rearrange("p (a d) -> p a d", a=1).broadcast_to([P, 2, D])
                    ins = nc.vector.tensor_tensor(tmp[:, 2 * k:2 * k + 2, :],
                                                  prod[:, k, :].rearrange("p (a d) -> p a d", d=D), g, ALU.mult)
                    if k == 1:
                        ins.then_inc(a_free, 1)
                    else:
                        then(ins)
                dve.wait_ge(a_free, s.a + 1)
                settled()
                xs = X[:, s.b * TT:(s.b + 1) * TT, :]
                add = nc.vector.tensor_tensor(xs, xs, tmp[:, :, :], ALU.add)
                if last_use:
                    add.then_inc(x_done, 1)
                else:
                    then(add)
                    settled()
                    stats(s.b)

            copies = 0
            for s in plan:
                if s.kind == "stats":
                    dve.wait_ge(x_in, 16)
                    stats(s.b)
                elif s.kind == "attend" and s.m is not None:
                    l, b, g = UNITS[s.m // TT]
                    qt = s.m % TT
                    n = P * (qt + 1) if l == 0 else T
                    if s.m == 0:
                        dve.wait_ge(cleared, 1)
                    for jj in range(2):
                        dve.wait_ge(a_ready, s.a + jj + 1)
                        if qt == 0 and jj == 0:
                            settled()
                            if s.m >= TT:
                                dve.wait_ge(mrow_ok, s.m // TT)
                        nc.vector.reduce_max(mx[:, qt, 2 * jj:2 * jj + 2], ringA[:, (s.a + jj) % 2, :, 0:n],
                                             AX_X).then_inc(a_free, 1)
                    if qt == TT - 1:
                        dve.wait_ge(a_free, s.a + 2)
                        if s.m // TT >= 1:
                            dve.wait_ge(a_ready, shift_job[s.m // TT - 1] + 1)
                        cols = mrow[:, :, :].rearrange("p t (j c) -> p t j c", c=PADD)
                        then(nc.vector.tensor_scalar(cols[:, :, :, MROW], mx[:, :, :], -1.0, None, ALU.mult))
                        settled()
                        nc.vector.scalar_tensor_tensor(out=cols[:, :, :, MROW + 1], in0=mx[:, :, :], scalar=-1.0,
                                                       in1=cols[:, :, :, MROW], op0=ALU.mult,
                                                       op1=ALU.subtract).then_inc(mrow_ok, 1)
                elif s.kind == "shift":
                    l, b, g = UNITS[s.u]
                    dve.wait_ge(a_ready, s.a + 1)
                    nc.vector.tensor_tensor(Qs[:, b, g, :], ringA[:, s.a % 2, 0, :], Qs[:, b, g, :].bitcast(F32),
                                            ALU.add).then_inc(a_free, 1)
                elif s.kind == "qk":
                    dve.wait_ge(rounded, s.n + 1)
                    dst = (Ks if s.side else Qs)[:, s.b, 2 * s.gp:2 * s.gp + 2, :]
                    nc.vector.scalar_tensor_tensor(out=dst, in0=part[:, :, :].bitcast(F32),
                                                   scalar=consts[:, s.side:s.side + 1],
                                                   in1=ringA[:, s.a % 2, :, :], op0=ALU.mult,
                                                   op1=ALU.add).then_inc(a_free, 1)
                elif s.kind == "copy":
                    dve.wait_ge(pv_done, 8 * (copies + 1))
                    settled()
                    if copies:
                        dve.wait_ge(norm_ok, TT * copies)
                    nc.vector.tensor_copy(ctxS[:, :], ctxP[:, :]).then_inc(ctx_free, 1)
                    copies += 1
                    dve.wait_ge(ctx_free, copies)
                elif s.kind == "norm":
                    cols = slice(s.p * P, (s.p + 1) * P)
                    mask = [SUM + 1 if HD <= i < 2 * HD or i == SUM + 1 else SUM for i in range(PADD)]
                    if s.n:
                        dve.wait_ge(norm_ok, s.n)
                    then(nc.vector.stream_shuffle(sums[:, :], ctxS[:, cols], mask))
                    settled()
                    then(nc.vector.reciprocal(rsum[:, :], sums[:, :]))
                    settled()
                    nc.vector.tensor_tensor(ctxN[:, s.gg, cols], ctxS[:, cols], rsum[:, :],
                                            ALU.mult).then_inc(norm_ok, 1)
                elif s.kind == "proj":
                    residual(s, 0, False)
                elif s.kind == "w2":
                    residual(s, 1, s.l == LAYERS - 1)

        @block.tensor
        def _(pe):
            def mm(out_, lhsT, rhs, start, stop):
                return nc.tensor.matmul(out_, lhsT, rhs, start=start, stop=stop)

            pe.wait_ge(silu_b, 1)
            pe.wait_ge(silu_c, 2)
            pe.wait_ge(ada_in, n_ada[0])
            VARS = (0, 1, 3, 4)
            for l in range(LAYERS):
                r0 = PADD * l
                if l > 0:
                    pe.wait_ge(mod_mm, l)
                for v in range(4):
                    c0 = VARS[v] * D
                    at = (l * 4 + v) * B
                    mm(ringA[:, 0, 0, at:at + B], ada[:, l, c0:c0 + P], sT[:, :], True, False)
                    mm(ringA[:, 0, 0, at:at + B], adar[r0:r0 + DREM + 1, c0:c0 + P], sR[r0:r0 + DREM + 1, :],
                       False, True)
                    m3 = ada3[:, l, v * 3 * DREM:(v + 1) * 3 * DREM]
                    r3 = adar3[r0:r0 + DREM + 1, v * 3 * DREM:(v + 1) * 3 * DREM]
                    mm(ringA[0:3 * DREM, 0, 1, at:at + B], m3, sT[:, :], True, False)
                    mm(ringA[0:3 * DREM, 0, 1, at:at + B], r3, sR[r0:r0 + DREM + 1, :], False, True)
                for h in range(2):
                    for b in range(B):
                        c0 = (2 + 3 * h) * D
                        o = gate_out(l, h, b)
                        mm(o, sTb[:, b, :], ada[:, l, c0:c0 + D], True, False)
                        last = mm(o, sRb[r0:r0 + DREM + 1, b, :], adar[r0:r0 + DREM + 1, c0:c0 + D], False, True)
                last.then_inc(mod_mm, 1)
            pe.wait_ge(mod_ok, 2)
            pe.wait_ge(consts_ok, 1)

            def claim_a(job):
                if job >= 2:
                    pe.wait_ge(a_free, job - 1)

            def claim_b(job):
                if job >= 3:
                    pe.wait_ge(b_free, job - 2)

            def weights(s):
                pe.wait_ge(w_ok, s.l + 1)
                pe.wait_ge(w_in[s.l], n_w[s.l])

            for s in plan:
                if s.kind == "shift":
                    claim_a(s.a)
                    pe.wait_ge(mrow_ok, s.u + 1)
                    for qt in range(TT):
                        last = mm(ringA[:, s.a % 2, 0, qt * P:(qt + 1) * P], mrow[:, qt, :], identb[:, :], True, True)
                    last.then_inc(a_ready, 1)
                elif s.kind == "attend":
                    def score_t(j):
                        l, b, g = UNITS[s.e // TT]
                        kt = s.e % TT
                        job = s.bj + j
                        rows = slice(PADD * j, PADD * j + MROW + 2)
                        q0 = span(l, kt)
                        base = min(q0, T - 2 * P)
                        claim_b(job)
                        if kt == 0 and j == 0:
                            pe.wait_ge(a_free, shift_job[s.e // TT] + 1)
                        last = mm(ringB[:, job % 3, 0:T - base], Ks[rows, b, g, kt * P:(kt + 1) * P],
                                  Qs[rows, b, g, base:T], True, l > 0)
                        if l == 0:
                            last = mm(ringB[:, job % 3, q0 - base:q0 - base + P], identb[:, :], maskT[:, :],
                                      False, True)
                        last.then_inc(b_ready, 1)

                    def score(jj):
                        l, b, g = UNITS[s.m // TT]
                        qt = s.m % TT
                        job = s.a + jj
                        n = max(P * (qt + 1), 2 * P) if l == 0 else T
                        claim_a(job)
                        if qt == 0 and jj == 0:
                            pe.wait_ge(a_free, max(qk_job[l, b, 0, g // 2].a, qk_job[l, b, 1, g // 2].a) + 1)
                        for i in range(2):
                            j = 2 * jj + i
                            rows = slice(PADD * j, PADD * j + SROWS)
                            last = mm(ringA[:, job % 2, i, 0:n], Qs[rows, b, g, qt * P:(qt + 1) * P],
                                      Ks[rows, b, g, 0:n], True, l > 0)
                            if l == 0:
                                last = mm(ringA[:, job % 2, i, qt * P:(qt + 1) * P], identb[:, :], maskS[:, :],
                                          False, True)
                        last.then_inc(a_ready, 1)

                    def weigh():
                        e = s.t - 1
                        l, b, g = UNITS[e // TT]
                        kt = e % TT
                        q0 = span(l, kt)
                        pe.wait_ge(b_free, exps_before[e])
                        if kt == 0 and g == 0:
                            pe.wait_ge(b_free, v_job[l, b].bj + 2)
                        if kt == 0 and g % 2 == 0 and e >= 8:
                            pe.wait_ge(ctx_free, e // 8)
                        for j in range(QUAD):
                            last = mm(ctxP[PADD * j:PADD * (j + 1), q0:T], V[:, b, kt, QUAD * g + j, :],
                                      probs[:, QUAD * (e % 2) + j, q0:T], g % 2 == 0 and kt == 0,
                                      g % 2 == 1 and kt == TT - 1)
                        last.then_inc(pv_done, 1)

                    if s.e is not None:
                        score_t(0)
                        score_t(1)
                    if s.m is not None:
                        score(0)
                    if s.e is not None:
                        score_t(2)
                    if 1 <= s.t <= QUARTERS:
                        weigh()
                    if s.e is not None:
                        score_t(3)
                    if s.m is not None:
                        score(1)
                elif s.kind == "proj":
                    claim_a(s.a)
                    weights(s)
                    pe.wait_ge(norm_ok, 2 * TT * (s.n + 1))
                    for tt in range(TT):
                        o = ringA[:, s.a % 2, tt // 2, (tt % 2) * D:(tt % 2 + 1) * D]
                        for gg in range(2):
                            last = mm(o, ctxN[:, gg, tt * P:(tt + 1) * P], w_p[:, s.l, gg, :], gg == 0, gg == 1)
                    last.then_inc(a_ready, 1)
                elif s.kind == "spread":
                    pe.wait_ge(xhat_ok, s.n + 1)
                    for i, (c0, rows) in enumerate(((0, P), (P, REM))):
                        claim_b(s.bj + i)
                        for tt in range(TT):
                            last = nc.tensor.transpose(ringB[0:rows, (s.bj + i) % 3, tt * P:(tt + 1) * P],
                                                       xe[:, tt, c0:c0 + rows], ident[:, :])
                        last.then_inc(b_ready, 1)
                elif s.kind == "qk":
                    claim_a(s.a)
                    weights(s)
                    ln = ln_job[s.l, s.b, 0]
                    pe.wait_ge(b_free, ln.bj + 1)
                    pe.wait_ge(hrem_ok, ln.n + 1)
                    for i in range(2):
                        g = 2 * s.gp + i
                        mm(ringA[:, s.a % 2, i, :], w_qk[:, s.l % 2, s.side, g, :], hmain[:, :], True, False)
                        last = mm(ringA[:, s.a % 2, i, :], r_qk[:, s.l % 2, s.side, g, :], hrem[:, :], False, True)
                    last.then_inc(a_ready, 1)
                elif s.kind == "v":
                    for i in range(2):
                        claim_b(s.bj + i)
                        for k in range(2):
                            tt = 2 * i + k
                            o = ringB[:, (s.bj + i) % 3, k * D:(k + 1) * D]
                            mm(o, hmain[:, tt * P:(tt + 1) * P], w_v[:, s.l, :], True, False)
                            last = mm(o, hrem[:, tt * P:(tt + 1) * P], r_vw[:, s.l, 0:D], False, True)
                        last.then_inc(b_ready, 1)
                elif s.kind == "w1":
                    ln = ln_job[s.l, s.b, 1]
                    weights(s)
                    pe.wait_ge(b_free, ln.bj + 1)
                    pe.wait_ge(hrem_ok, ln.n + 1)
                    for m in range(HT):
                        rows = P if m < HT - 1 else HLAST
                        claim_b(s.bj + m)
                        o = ringB[0:rows, (s.bj + m) % 3, :]
                        mm(o, w_1[:, s.l, m * P:m * P + rows], hmain[:, :], True, False)
                        last = mm(o, r_vw[:, s.l, D + m * P:D + m * P + rows], hrem[:, :], False, True)
                        last.then_inc(b_ready, 1)
                elif s.kind == "w2":
                    claim_a(s.a)
                    pe.wait_ge(b_free, w1_job[s.l, s.b].bj + HT)
                    for tt in range(TT):
                        o = ringA[:, s.a % 2, tt // 2, (tt % 2) * D:(tt % 2 + 1) * D]
                        for k in range(HT):
                            rows = P if k < HT - 1 else HLAST + 1
                            last = mm(o, hid[0:rows, k, tt * P:(tt + 1) * P], w_2[0:rows, s.l, k, :],
                                      k == 0, k == HT - 1)
                    last.then_inc(a_ready, 1)


def kernel(**inputs):
    import numpy as np
    import concourse.bacc as bacc
    from concourse.bass_utils import run_bass_kernel_spmd as run

    I = {name: np.asarray(a) for name, a in inputs.items()}
    none = np.zeros(3 * D, np.float32)
    qkv = [np.concatenate([I["L0_cond_W" + c] for c in "qkv"], 1), I["L1_cond_w_qkv"], I["L2_cond_W_qkv"],
           np.concatenate([I["L3_cond_w" + c] for c in "qkv"], 1)]
    b_qkv = [none, I["L1_cond_b_qkv"], I["L2_cond_b_qkv"], none]
    w1 = [I["L0_cond_W1"], I["L1_cond_w_fc1"], I["L2_cond_W_fc1"], I["L3_cond_fc1_w"]]
    b1 = [I["L0_cond_b1"], I["L1_cond_b_fc1"], I["L2_cond_b_fc1"], I["L3_cond_fc1_b"]]
    w2 = [I["L0_cond_W2"], I["L1_cond_w_fc2"], I["L2_cond_W_fc2"], I["L3_cond_fc2_w"]]
    b2 = [I["L0_cond_b2"], I["L1_cond_b_fc2"], I["L2_cond_b_fc2"], I["L3_cond_fc2_b"]]
    wp = [I["L0_cond_Wp"], I["L1_cond_w_proj"], I["L2_cond_W_proj"], I["L3_cond_wo"]]
    bp = [I["L0_cond_bp"], I["L1_cond_b_proj"], I["L2_cond_b_proj"], I["L3_cond_wo_b"]]
    wa = [I["L0_cond_Wa"], I["L1_cond_w_ada"], I["L2_cond_W_ada"], I["L3_cond_ada_w"]]
    ba = [I["L0_cond_ba"], I["L1_cond_b_ada"], I["L2_cond_b_ada"], I["L3_cond_ada_b"]]

    all1 = [np.concatenate([a, b], 1) for a, b in zip(qkv, w1)]
    bias1 = [np.concatenate([a, b]) for a, b in zip(b_qkv, b1)]
    w_main = np.stack([a[0:P] for a in all1])
    w_rem = np.stack([np.concatenate([a[P:D]] * 3 + [v[None]] * 2, 0) for a, v in zip(all1, bias1)])
    w_2 = np.zeros((LAYERS, P, HT, D), np.float32)
    w_p = np.zeros((LAYERS, P, 2, D), np.float32)
    ada_main = np.stack([a[0:P] for a in wa], 1)
    ada_rem = np.zeros((P, 6 * D), np.float32)
    c_rem = np.zeros((P, B), np.float32)
    for l in range(LAYERS):
        for k in range(HT):
            rows = w2[l][k * P:(k + 1) * P]
            w_2[l, 0:rows.shape[0], k] = rows
        w_2[l, HLAST, HT - 1] = b2[l]
        for h in range(HEADS):
            g, j = divmod(h, QUAD)
            at = PADD * j + HD * (g % 2)
            w_p[l, at:at + HD, g // 2] = wp[l][h * HD:(h + 1) * HD]
        w_p[l, SUM, 0] = bp[l]
        ada_rem[PADD * l:PADD * l + DREM] = wa[l][P:D]
        ada_rem[PADD * l + DREM] = ba[l]
        c_rem[PADD * l:PADD * l + DREM] = I["cond_1152"].T[P:D]
    thrice = [v * D + P + i for v in (0, 1, 3, 4) for _ in range(3) for i in range(DREM)]
    ln = np.stack([I["L3_cond_ln1_b"], I["L3_cond_ln1_w"], I["L3_cond_ln2_b"], I["L3_cond_ln2_w"]], 1)
    ln_rem = np.concatenate([ln[P:D]] * 3 + [np.zeros((2, 4), np.float32)], 0)

    consts = np.zeros((P, NC), np.float32)
    for j in range(QUAD):
        consts[PADD * j + 2 * HD:PADD * j + 3 * HD, 0] = -1.0
        consts[PADD * j + HD:PADD * j + 2 * HD, 1] = -1.0
    consts[2 * DREM:3 * DREM, 2] = -1.0
    consts[DREM:2 * DREM, 3] = -1.0
    consts[3 * DREM + 1, 3] = -1.0
    for l in range(LAYERS):
        consts[PADD * l:PADD * l + DREM, 4] = 1.0
        consts[PADD * l + DREM, 5] = 1.0
    kones = np.zeros((REM, PADD - SROWS), np.float32)
    kones[3 * DREM, 0:2] = 1.0
    modones = np.zeros((2, LAYERS, 4, B), np.float32)
    modones[:, :, 0::2, :] = 1.0

    nc = bacc.Bacc("TRN2", target_bir_lowering=False, num_devices=1)
    arrays, args = {}, {}
    for name, a in {"x": I["x"], "c_main": I["cond_1152"].T[0:P], "c_rem": c_rem, "ln_main": ln[0:P],
                    "ln_rem": ln_rem, "w_main": w_main, "w_rem": w_rem, "w_2": w_2, "w_p": w_p,
                    "ada_main": ada_main, "ada_rem": ada_rem,
                    "ada3_main": ada_main[:, :, thrice], "ada3_rem": ada_rem[:, thrice], "consts": consts, "kones": kones,
                    "modones": modones.reshape(2, LAYERS * 4 * B)}.items():
        a = np.ascontiguousarray(a)
        arrays[f"in_{name}"] = a
        args[name] = nc.dram_tensor(f"in_{name}", a.shape, mybir.dt.from_np(a.dtype), kind="ExternalInput").ap()
    out = nc.dram_tensor("out_x", (B, T, D), F32, kind="ExternalOutput").ap()
    program(nc, args, out)
    return run(nc, [arrays], core_ids=[0]).results[0]["out_x"]
```

```python
from contextlib import ExitStack

import concourse.bass as bass
from concourse import mybir

F32 = mybir.dt.float32
F32R = mybir.dt.float32r
BF16 = mybir.dt.bfloat16
ACT = mybir.ActivationFunctionType
ALU = mybir.AluOpType
AX_X = mybir.AxisListType.X

P = 128
LAYERS = 4
B, T, D = 2, 512, 144
HEADS = 16
HD = D // HEADS
HID = 4 * D
TT = T // P
QUAD = 4
GROUPS = HEADS // QUAD
DREM = D - P
REM = 3 * DREM + 2
SROWS = 3 * HD
MROW = SROWS
PADD = 32
SUM = 2 * HD
HT = -(-HID // P)
HLAST = HID - (HT - 1) * P
LEAD = 5
UNITS = [(l, b, g) for l in range(LAYERS) for b in range(B) for g in range(GROUPS)]
QUARTERS = TT * len(UNITS)
EPS = (1e-6, 1e-6, 1e-6, 1e-5)
MLP_FUNC = (ACT.Silu, ACT.Gelu_apprx_tanh, ACT.Gelu_apprx_tanh, ACT.Gelu)
NEG = -1e30
NC = 8
SCALE = HD ** -0.5


class Step:

    def __init__(self, kind, a, bj, n, l=0, b=0, half=0, side=0, gp=0, gg=0, p=0, u=0, t=0, e=None, m=None,
                 norm=None):
        self.kind, self.a, self.bj, self.n = kind, a, bj, n
        self.l, self.b, self.half = l, b, half
        self.side, self.gp, self.gg, self.p = side, gp, gg, p
        self.u, self.t, self.e, self.m = u, t, e, m
        self.norm = norm


def make_plan():
    plan = []
    jobs = {"a": 0, "b": 0}
    made = {}

    def add(kind, a=0, bb=0, **k):
        plan.append(Step(kind, jobs["a"], jobs["b"], made.get(kind, 0), **k))
        jobs["a"] += a
        jobs["b"] += bb
        made[kind] = made.get(kind, 0) + 1

    def chain(l, b):
        at = {0: [("copy", dict(b=b, gg=1)), ("norm", dict(b=b, gg=1, p=0)), ("norm", dict(b=b, gg=1, p=1))],
              1: [("norm", dict(b=b, gg=1, p=2)), ("norm", dict(b=b, gg=1, p=3))],
              2: [("proj", dict(a=1, l=l, b=b))],
              3: [("spread", dict(bb=2, l=l, b=b, half=1))],
              4: [("w1", dict(bb=HT, l=l, b=b))],
              5: [("w2", dict(a=1, l=l, b=b))]}
        if l + 1 < LAYERS:
            at.update(entry(l + 1, b))
        return at

    def entry(l, b):
        return {6: [("spread", dict(bb=2, l=l, b=b, half=0))],
                7: [("qk", dict(a=1, l=l, b=b, side=1, gp=0))],
                8: [("qk", dict(a=1, l=l, b=b, side=0, gp=0))],
                10: [("v", dict(bb=2, l=l, b=b)), ("qk", dict(a=1, l=l, b=b, side=1, gp=1))],
                11: [("qk", dict(a=1, l=l, b=b, side=0, gp=1))]}

    add("stats", b=0)
    for steps in entry(0, 0).values():
        for kind, k in steps:
            add(kind, **k)
    dense = {-2: [("stats", dict(b=1))]}
    for k, v in entry(0, 1).items():
        dense.setdefault(k - 4, []).extend(v)
    for l in range(LAYERS):
        for b in range(B):
            own = 4 * GROUPS * (B * l + b)
            dense.setdefault(own + 8, []).extend(
                [("copy", dict(b=b, gg=0)), ("norm", dict(b=b, gg=0, p=0))])
            for p in (1, 2, 3):
                dense.setdefault(own + 8 + p, []).append(("norm", dict(b=b, gg=0, p=p)))
            for k, v in chain(l, b).items():
                dense.setdefault(own + 16 + k, []).extend(v)
    for t in range(-LEAD, max(max(dense) + 1, QUARTERS + 1)):
        if t >= -1 and t % TT == TT - 1 and t < QUARTERS - 1:
            add("shift", a=1, u=(t + 1) // TT)
        e = t if 0 <= t < QUARTERS else None
        m = t + LEAD if t + LEAD < QUARTERS else None
        spread = [k for kind, k in dense.get(t, []) if kind == "spread"]
        if e is not None or m is not None or t == QUARTERS:
            add("attend", a=0 if m is None else 2, bb=0 if e is None else QUAD, t=t, e=e, m=m,
                norm=spread[0] if spread and m is not None else None)
        for kind, k in dense.get(t, []):
            add(kind, **k)
    return plan


def span(l, tile):
    return P * tile if l == 0 else 0


def program(nc, A, out):
    plan = make_plan()
    ctx = ExitStack()
    with ctx:
        def sb(name, shape, dt=F32):
            return ctx.enter_context(nc.sbuf_tensor(name, shape, dt))

        def sem(name):
            return ctx.enter_context(nc.semaphore(name))

        X = sb("X", [P, B * TT, D])
        w_qk = sb("w_qk", [P, 2, 2, GROUPS, P])
        r_qk = sb("r_qk", [REM, 2, 2, GROUPS, P], F32R)
        raw_qk = sb("raw_qk", [P, 2 * D])
        w_v = sb("w_v", [P, LAYERS, D])
        w_1 = sb("w_1", [P, 2, HID])
        NR = 3 * D + HID
        raw_r = sb("raw_r", [REM, NR])
        r_mu = sb("r_mu", [REM, NR])
        r_vw = sb("r_vw", [REM, 2, D + HID], F32R)
        w_2 = sb("w_2", [P, LAYERS, HT, D])
        w_p = sb("w_p", [P, LAYERS, 2, D])
        cT = sb("cT", [P, B])
        cR = sb("cR", [P, B])
        sT = sb("sT", [P, B])
        sR = sb("sR", [P, B])
        sTb = sb("sTb", [P, B, P])
        sRb = sb("sRb", [P, B, P])
        mod = sb("mod", [P, LAYERS, 4, B])
        modr = sb("modr", [REM, LAYERS, 4, B])
        lnw = sb("lnw", [P, 4])
        lnwr = sb("lnwr", [REM, 4])
        gate = sb("gate", [P, LAYERS, 2, B, D])
        consts = sb("consts", [P, NC])
        kones = sb("kones", [REM, PADD - SROWS])
        ident = sb("ident", [P, P])
        identb = sb("identb", [P, P], BF16)
        maskS = sb("maskS", [P, P], BF16)
        maskT = sb("maskT", [P, P], BF16)
        half = sb("half", [P, TT + 1])
        Qs = sb("Qs", [P, B, GROUPS, T], F32R)
        Ks = sb("Ks", [P, B, GROUPS, T], F32R)
        Qz = sb("Qz", [P, 2, QUAD, T], F32R)
        Kz = sb("Kz", [P, 2, QUAD, T], F32R)
        V = sb("V", [P, B, TT, HEADS, PADD])
        probs = sb("probs", [P, 2 * QUAD, T])
        ada = probs[:, :, :].rearrange("p a b -> p (a b)")[:, 0:LAYERS * 6 * D].rearrange(
            "p (l n) -> p l n", l=LAYERS)
        part = sb("part", [P, 2, T], F32R)
        mx = sb("mx", [P, TT, QUAD])
        mrow = sb("mrow", [P, TT, P], BF16)
        ctxS = sb("ctxS", [P, T])
        ctxN = sb("ctxN", [P, 2, T])
        adar = ctxN[:, :, :].rearrange("p a b -> p (a b)")[:, 0:6 * D]
        sums = sb("sums", [P, P])
        rsum = sb("rsum", [P, P])
        tmp = sb("tmp", [P, TT, D])
        st = sb("st", [P, TT, 6])
        mv = sb("mv", [P, TT, 2])
        ve = sb("ve", [P, TT])
        rstd = sb("rstd", [P, TT])
        XE = 180
        xe = sb("xe", [P, TT, XE])
        hmain = sb("hmain", [P, T])
        yrem = sb("yrem", [REM, T])
        hrnd = sb("hrnd", [REM, T], F32R)
        hrem = sb("hrem", [REM, T], F32R)
        hid = sb("hid", [P, HT, T])
        N3 = 4 * 3 * DREM
        hid_flat = hid[:, :, :].rearrange("p a b -> p (a b)")
        ada3 = hid_flat[:, 0:LAYERS * N3].rearrange("p (l n) -> p l n", l=LAYERS)
        adar3 = hid_flat[:, LAYERS * N3:(LAYERS + 1) * N3]

        ringA = ctx.enter_context(nc.psum_tensor("ringA", [P, 2, 2, T], F32))
        ringB = ctx.enter_context(nc.psum_tensor("ringB", [P, 3, T], F32))
        ctxP = ctx.enter_context(nc.psum_tensor("ctxP", [P, T], F32))

        def gate_out(l, h, b):
            bank, at = divmod((l * 2 + h) * B + b, 3)
            where = (ringA[:, 1, 0, :], ringA[:, 1, 1, :], ringB[:, 0, :], ringB[:, 1, :], ringB[:, 2, :],
                     ctxP[:, :])[bank]
            return where[:, at * D:(at + 1) * D]

        small_in = sem("small_in")
        x_in = sem("x_in")
        w_in = [sem(f"w_in{l}") for l in range(LAYERS)]
        raw_in = sem("raw_in")
        ada_in = sem("ada_in")
        cleared = sem("cleared")
        consts_ok = sem("consts_ok")
        pool_ops = sem("pool_ops")
        dve_ops = sem("dve_ops")
        silu_c = sem("silu_c")
        silu_b = sem("silu_b")
        mod_mm = sem("mod_mm")
        mod_read = sem("mod_read")
        mod_ok = sem("mod_ok")
        w_ok = sem("w_ok")
        a_ready, a_free = sem("a_ready"), sem("a_free")
        b_ready, b_free = sem("b_ready"), sem("b_free")
        rounded = sem("rounded")
        apart_zero = sem("apart_zero")
        qz_in = [sem(f"qz_in{i}") for i in range(2)]
        kz_in = [sem(f"kz_in{i}") for i in range(2)]
        mrow_ok = sem("mrow_ok")
        pv_done = sem("pv_done")
        ctx_free = sem("ctx_free")
        norm_ok = sem("norm_ok")
        stats_ok = sem("stats_ok")
        rstd_ok = sem("rstd_ok")
        xhat_ok = sem("xhat_ok")
        hrem_ok = sem("hrem_ok")
        x_done = sem("x_done")
        stored = sem("stored")

        exps_before = {}
        for s in plan:
            if s.kind == "attend" and s.e is not None:
                exps_before[s.e] = s.bj + QUAD
        attend_m = {s.m: s for s in plan if s.kind == "attend" and s.m is not None}
        shift_job = {s.u: s.a for s in plan if s.kind == "shift"}
        qk_job = {(s.l, s.b, s.side, s.gp): s for s in plan if s.kind == "qk"}
        v_job = {(s.l, s.b): s for s in plan if s.kind == "v"}
        ln_job = {(s.l, s.b, s.half): s for s in plan if s.kind == "spread"}
        w1_job = {(s.l, s.b): s for s in plan if s.kind == "w1"}
        qk_steps = [s for s in plan if s.kind == "qk"]
        ln_steps = [s for s in plan if s.kind == "spread"]

        n_w = [0] * LAYERS
        n_raw = [0] * LAYERS
        n_small = [0]
        block = ctx.enter_context(nc.Block())

        def load(eng, semaphore, dst, src, counter, i=0):
            eng.dma_start(dst, src).then_inc(semaphore, 16)
            counter[i] += 16

        n_ada = [0]

        def load_raw(eng, l):
            if l > 0:
                eng.wait_ge(w_ok, l)
            load(eng, raw_in, raw_qk[:, :], A["w_main"][l, :, 0:2 * D], n_raw, l)
            load(eng, raw_in, raw_r[:, :], A["w_rem"][l], n_raw, l)

        def load_w1(eng, l):
            if l >= 2:
                eng.wait_ge(b_ready, w1_job[l - 2, B - 1].bj + HT)
            load(eng, w_in[l], w_1[:, l % 2, :], A["w_main"][l, :, 3 * D:NR], n_w, l)

        def load_rest(eng, l):
            load(eng, w_in[l], w_v[:, l, :], A["w_main"][l, :, 2 * D:3 * D], n_w, l)
            load(eng, w_in[l], w_p[:, l, :, :], A["w_p"][l], n_w, l)
            load(eng, w_in[l], w_2[:, l, :, :], A["w_2"][l], n_w, l)

        @block.sync
        def _(sp):
            x_v = A["x"].rearrange("b (t p) d -> p (b t) d", p=P)
            sp.dma_start(X[:, :, :], x_v).then_inc(x_in, 16)
            load_raw(sp, 0)
            load_rest(sp, 0)
            load_w1(sp, 0)
            load(sp, ada_in, ada, A["ada_main"], n_ada)
            load(sp, ada_in, adar, A["ada_rem"], n_ada)
            load(sp, ada_in, ada3, A["ada3_main"], n_ada)
            load(sp, ada_in, adar3, A["ada3_rem"], n_ada)
            load_raw(sp, 1)
            load_w1(sp, 1)
            for l in range(1, LAYERS):
                load_rest(sp, l)

            def apart(what, u):
                l, b, g = UNITS[u]
                src, dst, sems, side = (Qs, Qz, qz_in, 0) if what == "q" else (Ks, Kz, kz_in, 1)
                sp.wait_ge(a_free, qk_job[l, b, side, g // 2].a + 1)
                if u < 2:
                    sp.wait_ge(apart_zero, 1)
                elif what == "q":
                    sp.wait_ge(a_ready, attend_m[4 * (u - 2) + 3].a + 2)
                else:
                    sp.wait_ge(b_ready, exps_before[4 * (u - 2) + 3])
                for j in range(QUAD):
                    rows = slice(PADD * j, PADD * (j + 1))
                    sp.dma_start(dst[rows, u % 2, j, :].bitcast(F32),
                                 src[rows, b, g, :].bitcast(F32)).then_inc(sems[u % 2], 16)

            apart("q", 0)
            for u in range(len(UNITS)):
                apart("k", u)
                if u + 1 < len(UNITS):
                    apart("q", u + 1)
                for l in range(2, LAYERS):
                    if u == B * GROUPS * (l - 2) + 2:
                        load_raw(sp, l)
                    if u == B * GROUPS * (l - 1) + 2:
                        load_w1(sp, l)
            out_v = out.rearrange("b (t p) d -> p (b t) d", p=P)
            for b in range(B):
                sp.wait_ge(x_done, b + 1)
                sp.dma_start(out_v[:, b * TT:(b + 1) * TT, :], X[:, b * TT:(b + 1) * TT, :]).then_inc(stored, 16)
            sp.wait_ge(stored, 16 * B)

        @block.scalar
        def _(act):
            load(act, small_in, cT[:, :], A["c_main"], n_small)
            load(act, small_in, cR[:, :], A["c_rem"], n_small)
            load(act, small_in, consts[:, :], A["consts"], n_small)
            load(act, small_in, kones[:, :], A["kones"], n_small)
            load(act, small_in, lnw[:, :], A["ln_main"], n_small)
            load(act, small_in, lnwr[:, :], A["ln_rem"], n_small)
            load(act, small_in, modr[3 * DREM:REM, :, :, :].rearrange("p a b c -> p (a b c)"),
                 A["modones"], n_small)
            act.wait_ge(small_in, n_small[0])
            nc.scalar.activation(sT[:, :], cT[:, :], ACT.Silu).then_inc(silu_c, 1)
            nc.scalar.activation(sR[:, :], cR[:, :], ACT.Silu).then_inc(silu_c, 1)

            for s in plan:
                if s.kind == "attend" and s.e is not None:
                    l, b, g = UNITS[s.e // TT]
                    kt = s.e % TT
                    q0 = span(l, kt)
                    base = min(q0, T - 2 * P)
                    for j in range(QUAD):
                        job = s.bj + j
                        act.wait_ge(b_ready, job + 1)
                        if s.e >= 2:
                            act.wait_ge(pv_done, s.e - 1)
                        nc.scalar.activation(probs[:, QUAD * (s.e % 2) + j, q0:T],
                                             ringB[:, job % 3, q0 - base:T - base],
                                             ACT.Exp, scale=SCALE).then_inc(b_free, 1)
                elif s.kind == "spread":
                    v0 = 2 * s.half
                    if s.n == 0:
                        act.wait_ge(mod_ok, 1)
                    act.wait_ge(b_ready, s.bj + 1)
                    nc.scalar.activation(hmain[:, :], ringB[:, s.bj % 3, :], ACT.Identity,
                                         scale=mod[:, s.l, v0 + 1, s.b:s.b + 1],
                                         bias=mod[:, s.l, v0, s.b:s.b + 1]).then_inc(b_free, 1)
                    act.wait_ge(b_ready, s.bj + 2)
                    if s.n >= 1:
                        act.wait_ge(hrem_ok, s.n)
                    for to in (yrem, hrnd):
                        last = nc.scalar.activation(to[:, :], ringB[0:REM, (s.bj + 1) % 3, :], ACT.Identity,
                                                    scale=modr[:, s.l, v0 + 1, s.b:s.b + 1],
                                                    bias=modr[:, s.l, v0, s.b:s.b + 1])
                    last.then_inc(b_free, 1)
                elif s.kind == "qk":
                    act.wait_ge(a_ready, s.a + 1)
                    if s.n >= 1:
                        act.wait_ge(a_free, qk_steps[s.n - 1].a + 1)
                    nc.scalar.activation(part[:, :, :], ringA[:, s.a % 2, :, :], ACT.Copy).then_inc(rounded, 1)
                elif s.kind == "v":
                    for i in range(2):
                        job = s.bj + i
                        act.wait_ge(b_ready, job + 1)
                        if s.n == 0 and i == 0:
                            act.wait_ge(cleared, 1)
                        for k in range(2):
                            tt = 2 * i + k
                            for gg in range(2):
                                src = ringB[:, job % 3, k * D + gg * 8 * HD:k * D + (gg + 1) * 8 * HD].rearrange(
                                    "p (s j d) -> p s j d", s=2, j=QUAD)
                                for sx in range(2):
                                    h0 = 8 * gg + QUAD * sx
                                    last = nc.scalar.activation(V[:, s.b, tt, h0:h0 + QUAD, HD * sx:HD * sx + HD],
                                                                src[:, sx], ACT.Copy)
                        last.then_inc(b_free, 1)
                elif s.kind == "w1":
                    for m in range(HT):
                        rows = P if m < HT - 1 else HLAST
                        act.wait_ge(b_ready, s.bj + m + 1)
                        nc.scalar.activation(hid[0:rows, m, :], ringB[0:rows, (s.bj + m) % 3, :],
                                             MLP_FUNC[s.l]).then_inc(b_free, 1)

        @block.gpsimd
        def _(pool):
            done = [0]

            def then(ins):
                done[0] += 1
                return ins.then_inc(pool_ops, 1)

            def settled():
                pool.wait_ge(pool_ops, done[0])

            then(nc.gpsimd.memset(half[:, :], -0.5))
            then(nc.gpsimd.memset(xe[:, :, D + 2 * DREM:XE], 0.0))
            for m in (ident, identb, maskS, maskT):
                then(nc.gpsimd.memset(m[:, :], 0.0))
            settled()
            for m in (ident, identb):
                then(nc.gpsimd.affine_select(out=m[:, :], in_=m[:, :], compare_op=ALU.not_equal, fill=1.0,
                                             base=0, pattern=[[-1, P]], channel_multiplier=1))
            then(nc.gpsimd.affine_select(out=maskS[:, :], in_=maskS[:, :], compare_op=ALU.is_ge, fill=NEG,
                                         base=0, pattern=[[-1, P]], channel_multiplier=1))
            then(nc.gpsimd.affine_select(out=maskT[:, :], in_=maskT[:, :], compare_op=ALU.is_ge, fill=NEG,
                                         base=0, pattern=[[1, P]], channel_multiplier=-1))
            settled()
            nc.gpsimd.memset(hid[HLAST:HLAST + 1, HT - 1, :], 1.0).then_inc(consts_ok, 1)
            pool.wait_ge(consts_ok, 1)
            then(nc.gpsimd.memset(V[:, :, :, :, HD:PADD], 0.0))
            then(nc.gpsimd.memset(V[:, :, :, :, 0:HD], 0.0))
            settled()
            for b in range(B):
                for sx in range(2):
                    v = V[:, b, :, :, SUM + sx:SUM + sx + 1].rearrange("p t (g s j) c -> p s (t g) (j c)", g=2, s=2)
                    then(nc.gpsimd.memset(v[:, sx], 1.0))
            settled()
            nc.gpsimd.memset(mrow[:, :, :], 0.0).then_inc(cleared, 1)

            def stack_weights(l):
                pool.wait_ge(raw_in, 32 * (l + 1))
                if l == 0:
                    pool.wait_ge(small_in, n_small[0])
                if l >= 2:
                    pool.wait_ge(a_ready, qk_job[l - 2, B - 1, 0, 1].a + 1)
                    pool.wait_ge(b_ready, w1_job[l - 2, B - 1].bj + HT)
                settled()
                then(nc.gpsimd.tensor_copy(r_mu[:, :].bitcast(F32R), raw_r[:, :]))
                settled()
                then(nc.gpsimd.tensor_scalar(r_mu[:, :], r_mu[:, :], consts[0:REM, 3:4], None, ALU.mult))
                settled()
                then(nc.gpsimd.tensor_tensor(r_vw[:, l % 2, :], raw_r[:, 2 * D:NR], r_mu[:, 2 * D:NR], ALU.add))
                then(nc.gpsimd.tensor_tensor(raw_r[:, 0:2 * D], raw_r[:, 0:2 * D], r_mu[:, 0:2 * D], ALU.add))
                settled()
                for i in range(2):
                    for dst, raw in ((w_qk, raw_qk), (r_qk, raw_r)):
                        to = dst[:, l % 2, i].rearrange("p g (j c) -> p (g j) c", c=PADD)
                        frm = raw[:, i * D:(i + 1) * D].rearrange("p (h d) -> p h d", d=HD)
                        for r in range(3):
                            then(nc.gpsimd.tensor_copy(to[:, :, r * HD:(r + 1) * HD], frm))
                        pad = to[:, :, SROWS:PADD]
                        if dst is r_qk and i == 1:
                            ones = kones[:, :].rearrange("p (a c) -> p a c", a=1).broadcast_to(
                                [REM, HEADS, PADD - SROWS])
                            then(nc.gpsimd.tensor_copy(pad, ones))
                        elif dst is r_qk:
                            then(nc.gpsimd.memset(pad.bitcast(F32), 0.0))
                        else:
                            then(nc.gpsimd.memset(pad, 0.0))
                settled()
                nc.gpsimd.tensor_copy(half[:, TT:TT + 1], half[:, 0:1]).then_inc(w_ok, 1)

            stack_weights(0)
            for s in plan:
                if s.kind == "spread":
                    pool.wait_ge(stats_ok, s.n + 1)
                    if s.n >= 1:
                        pool.wait_ge(xhat_ok, s.n)
                    nc.gpsimd.tensor_tensor(rstd[:, :], ve[:, :], half[:, 0:TT], ALU.pow).then_inc(rstd_ok, 1)
                    if s.n == 0:
                        stack_weights(1)
                    elif s.b == B - 1 and s.half == 1 and s.l < LAYERS - 2:
                        stack_weights(s.l + 2)

        @block.vector
        def _(dve):
            done = [0]

            def then(ins):
                done[0] += 1
                return ins.then_inc(dve_ops, 1)

            def settled():
                dve.wait_ge(dve_ops, done[0])

            then(nc.vector.memset(Qz[:, :, :, :].bitcast(F32), 0.0))
            nc.vector.memset(Kz[:, :, :, :].bitcast(F32), 0.0).then_inc(apart_zero, 1)
            dve.wait_ge(silu_c, 2)
            dve.wait_ge(small_in, n_small[0])
            then(nc.vector.tensor_scalar(sR[:, :], sR[:, :], consts[:, 4:5], consts[:, 5:6], ALU.mult, ALU.add))
            settled()
            then(nc.vector.tensor_copy(sTb[:, :, :], sT[:, :].rearrange("p (b a) -> p b a", a=1).broadcast_to([P, B, P])))
            nc.vector.tensor_copy(sRb[:, :, :], sR[:, :].rearrange("p (b a) -> p b a", a=1).broadcast_to(
                [P, B, P])).then_inc(silu_b, 1)
            settled()
            dve.wait_ge(silu_b, 1)
            dve.wait_ge(mod_mm, LAYERS)
            src = ringA[:, 0, 0, 0:LAYERS * 4 * B].rearrange("p (l v b) -> p l v b", l=LAYERS, v=4)
            srcr = ringA[0:3 * DREM, 0, 1, 0:LAYERS * 4 * B].rearrange("p (l v b) -> p l v b", l=LAYERS, v=4)
            modc = modr[0:3 * DREM]
            for dst, frm in ((mod, src), (modc, srcr)):
                for h in range(2):
                    then(nc.vector.tensor_copy(dst[:, :, 2 * h, :], frm[:, :, 2 * h, :]))
                    then(nc.vector.tensor_scalar(dst[:, :, 2 * h + 1, :], frm[:, :, 2 * h + 1, :], 1.0, None, ALU.add))
            settled()
            for dst, wb in ((mod, lnw), (modc, lnwr[0:3 * DREM])):
                for h in range(2):
                    sh, sc = dst[:, LAYERS - 1, 2 * h, :], dst[:, LAYERS - 1, 2 * h + 1, :]
                    then(nc.vector.scalar_tensor_tensor(out=sh, in0=sc, scalar=wb[:, 2 * h:2 * h + 1], in1=sh,
                                                        op0=ALU.mult, op1=ALU.add))
                    settled()
                    then(nc.vector.tensor_scalar(sc, sc, wb[:, 2 * h + 1:2 * h + 2], None, ALU.mult))
            settled()
            nc.vector.memset(ctxS[:, 0:2], 0.0).then_inc(mod_ok, 1)
            for l in range(LAYERS):
                for h in range(2):
                    for b in range(B):
                        cp = nc.vector.tensor_copy(gate[:, l, h, b, :], gate_out(l, h, b))
                        if (l, h, b) == (LAYERS - 1, 1, B - 1):
                            cp.then_inc(mod_ok, 1)
                        else:
                            then(cp)
            dve.wait_ge(mod_ok, 2)
            settled()

            def stats(b, l):
                for tt in range(TT):
                    then(nc.vector.bn_stats(st[:, tt, :], X[:, b * TT + tt, :]))
                settled()
                for tt in range(TT):
                    then(nc.vector.bn_aggr(mv[:, tt, :], st[:, tt, :]))
                settled()
                nc.vector.tensor_scalar(ve[:, :], mv[:, :, 1], EPS[l], None, ALU.add).then_inc(stats_ok, 1)

            def normalise(s):
                dve.wait_ge(rstd_ok, s.n + 1)
                if s.n >= 1:
                    dve.wait_ge(b_ready, ln_steps[s.n - 1].bj + 2)
                for tt in range(TT):
                    x = X[:, s.b * TT + tt, :]
                    then(nc.vector.tensor_scalar(xe[:, tt, 0:P], x[:, 0:P], mv[:, tt, 0:1],
                                                 rstd[:, tt:tt + 1], ALU.subtract, ALU.mult))
                    rep = x[:, P:D].rearrange("p (a c) -> p a c", a=1).broadcast_to([P, 3, DREM])
                    last = nc.vector.tensor_scalar(
                        xe[:, tt, P:P + 3 * DREM].rearrange("p (a c) -> p a c", a=3), rep,
                        mv[:, tt, 0:1], rstd[:, tt:tt + 1], ALU.subtract, ALU.mult)
                    if tt < TT - 1:
                        then(last)
                last.then_inc(xhat_ok, 1)

            def residual(s, h, last_use):
                dve.wait_ge(a_ready, s.a + 1)
                prod = ringA[:, s.a % 2, :, 0:2 * D]
                for k in range(2):
                    g = gate[:, s.l, h, s.b, :].rearrange("p (a d) -> p a d", a=1).broadcast_to([P, 2, D])
                    ins = nc.vector.tensor_tensor(tmp[:, 2 * k:2 * k + 2, :],
                                                  prod[:, k, :].rearrange("p (a d) -> p a d", d=D), g, ALU.mult)
                    if k == 1:
                        ins.then_inc(a_free, 1)
                    else:
                        then(ins)
                dve.wait_ge(a_free, s.a + 1)
                settled()
                xs = X[:, s.b * TT:(s.b + 1) * TT, :]
                add = nc.vector.tensor_tensor(xs, xs, tmp[:, :, :], ALU.add)
                if last_use:
                    add.then_inc(x_done, 1)
                else:
                    then(add)
                    settled()
                    stats(s.b, s.l + h)

            normed = {ln_job[s.norm["l"], s.norm["b"], s.norm["half"]].n
                      for s in plan if s.kind == "attend" and s.norm}
            copies = 0
            for s in plan:
                if s.kind == "stats":
                    dve.wait_ge(x_in, 16)
                    stats(s.b, 0)
                elif s.kind == "attend" and s.m is not None:
                    l, b, g = UNITS[s.m // TT]
                    qt = s.m % TT
                    n = P * (qt + 1) if l == 0 else T
                    if s.m == 0:
                        dve.wait_ge(cleared, 1)
                    for jj in range(2):
                        dve.wait_ge(a_ready, s.a + jj + 1)
                        if qt == 0 and jj == 0:
                            settled()
                            if s.m >= TT:
                                dve.wait_ge(mrow_ok, s.m // TT)
                        nc.vector.reduce_max(mx[:, qt, 2 * jj:2 * jj + 2], ringA[:, (s.a + jj) % 2, :, 0:n],
                                             AX_X).then_inc(a_free, 1)
                        if jj == 0 and s.norm:
                            normalise(ln_job[s.norm["l"], s.norm["b"], s.norm["half"]])
                    if qt == TT - 1:
                        dve.wait_ge(a_free, s.a + 2)
                        if s.m // TT >= 1:
                            dve.wait_ge(a_ready, shift_job[s.m // TT - 1] + 1)
                        cols = mrow[:, :, :].rearrange("p t (j c) -> p t j c", c=PADD)
                        then(nc.vector.tensor_scalar(cols[:, :, :, MROW], mx[:, :, :], -1.0, None, ALU.mult))
                        settled()
                        nc.vector.scalar_tensor_tensor(out=cols[:, :, :, MROW + 1], in0=mx[:, :, :], scalar=-1.0,
                                                       in1=cols[:, :, :, MROW], op0=ALU.mult,
                                                       op1=ALU.subtract).then_inc(mrow_ok, 1)
                elif s.kind == "shift":
                    l, b, g = UNITS[s.u]
                    dve.wait_ge(a_ready, s.a + 1)
                    nc.vector.tensor_tensor(Qs[:, b, g, :], ringA[:, s.a % 2, 0, :], Qs[:, b, g, :].bitcast(F32),
                                            ALU.add).then_inc(a_free, 1)
                elif s.kind == "spread":
                    if s.n not in normed:
                        normalise(s)
                    dve.wait_ge(b_free, s.bj + 2)
                    nc.vector.scalar_tensor_tensor(out=hrem[:, :], in0=hrnd[:, :].bitcast(F32),
                                                   scalar=consts[0:REM, 2:3], in1=yrem[:, :],
                                                   op0=ALU.mult, op1=ALU.add).then_inc(hrem_ok, 1)
                elif s.kind == "qk":
                    dve.wait_ge(rounded, s.n + 1)
                    dst = (Ks if s.side else Qs)[:, s.b, 2 * s.gp:2 * s.gp + 2, :]
                    nc.vector.scalar_tensor_tensor(out=dst, in0=part[:, :, :].bitcast(F32),
                                                   scalar=consts[:, s.side:s.side + 1],
                                                   in1=ringA[:, s.a % 2, :, :], op0=ALU.mult,
                                                   op1=ALU.add).then_inc(a_free, 1)
                elif s.kind == "copy":
                    dve.wait_ge(pv_done, 8 * (copies + 1))
                    settled()
                    if copies:
                        dve.wait_ge(norm_ok, TT * copies)
                    nc.vector.tensor_copy(ctxS[:, :], ctxP[:, :]).then_inc(ctx_free, 1)
                    copies += 1
                    dve.wait_ge(ctx_free, copies)
                elif s.kind == "norm":
                    cols = slice(s.p * P, (s.p + 1) * P)
                    mask = [SUM + 1 if HD <= i < 2 * HD or i == SUM + 1 else SUM for i in range(PADD)]
                    if s.n:
                        dve.wait_ge(norm_ok, s.n)
                    then(nc.vector.stream_shuffle(sums[:, :], ctxS[:, cols], mask))
                    settled()
                    then(nc.vector.reciprocal(rsum[:, :], sums[:, :]))
                    settled()
                    nc.vector.tensor_tensor(ctxN[:, s.gg, cols], ctxS[:, cols], rsum[:, :],
                                            ALU.mult).then_inc(norm_ok, 1)
                elif s.kind == "proj":
                    residual(s, 0, False)
                elif s.kind == "w2":
                    residual(s, 1, s.l == LAYERS - 1)

        @block.tensor
        def _(pe):
            def mm(out_, lhsT, rhs, start, stop):
                return nc.tensor.matmul(out_, lhsT, rhs, start=start, stop=stop)

            pe.wait_ge(silu_b, 1)
            pe.wait_ge(silu_c, 2)
            pe.wait_ge(ada_in, n_ada[0])
            VARS = (0, 1, 3, 4)
            for l in range(LAYERS):
                r0 = PADD * l
                if l > 0:
                    pe.wait_ge(mod_mm, l)
                for v in range(4):
                    c0 = VARS[v] * D
                    at = (l * 4 + v) * B
                    mm(ringA[:, 0, 0, at:at + B], ada[:, l, c0:c0 + P], sT[:, :], True, False)
                    mm(ringA[:, 0, 0, at:at + B], adar[r0:r0 + DREM + 1, c0:c0 + P], sR[r0:r0 + DREM + 1, :],
                       False, True)
                    m3 = ada3[:, l, v * 3 * DREM:(v + 1) * 3 * DREM]
                    r3 = adar3[r0:r0 + DREM + 1, v * 3 * DREM:(v + 1) * 3 * DREM]
                    mm(ringA[0:3 * DREM, 0, 1, at:at + B], m3, sT[:, :], True, False)
                    mm(ringA[0:3 * DREM, 0, 1, at:at + B], r3, sR[r0:r0 + DREM + 1, :], False, True)
                for h in range(2):
                    for b in range(B):
                        c0 = (2 + 3 * h) * D
                        o = gate_out(l, h, b)
                        mm(o, sTb[:, b, :], ada[:, l, c0:c0 + D], True, False)
                        last = mm(o, sRb[r0:r0 + DREM + 1, b, :], adar[r0:r0 + DREM + 1, c0:c0 + D], False, True)
                last.then_inc(mod_mm, 1)
            pe.wait_ge(mod_ok, 2)
            pe.wait_ge(consts_ok, 1)

            def claim_a(job):
                if job >= 2:
                    pe.wait_ge(a_free, job - 1)

            def claim_b(job):
                if job >= 3:
                    pe.wait_ge(b_free, job - 2)

            def weights(s):
                pe.wait_ge(w_ok, s.l + 1)
                pe.wait_ge(w_in[s.l], n_w[s.l])

            for s in plan:
                if s.kind == "shift":
                    claim_a(s.a)
                    pe.wait_ge(mrow_ok, s.u + 1)
                    for qt in range(TT):
                        last = mm(ringA[:, s.a % 2, 0, qt * P:(qt + 1) * P], mrow[:, qt, :], identb[:, :], True, True)
                    last.then_inc(a_ready, 1)
                elif s.kind == "attend":
                    def score_t(j):
                        l, b, g = UNITS[s.e // TT]
                        kt = s.e % TT
                        job = s.bj + j
                        unit = s.e // TT
                        q0 = span(l, kt)
                        base = min(q0, T - 2 * P)
                        claim_b(job)
                        if kt == 0 and j == 0:
                            pe.wait_ge(a_free, shift_job[unit] + 1)
                            pe.wait_ge(kz_in[unit % 2], 16 * QUAD * (unit // 2 + 1))
                        last = mm(ringB[:, job % 3, 0:T - base], Kz[:, unit % 2, j, kt * P:(kt + 1) * P],
                                  Qs[:, b, g, base:T], True, l > 0)
                        if l == 0:
                            last = mm(ringB[:, job % 3, q0 - base:q0 - base + P], identb[:, :], maskT[:, :],
                                      False, True)
                        last.then_inc(b_ready, 1)

                    def score(jj):
                        l, b, g = UNITS[s.m // TT]
                        qt = s.m % TT
                        unit = s.m // TT
                        job = s.a + jj
                        n = max(P * (qt + 1), 2 * P) if l == 0 else T
                        claim_a(job)
                        if qt == 0 and jj == 0:
                            pe.wait_ge(a_free, max(qk_job[l, b, 0, g // 2].a, qk_job[l, b, 1, g // 2].a) + 1)
                            pe.wait_ge(qz_in[unit % 2], 16 * QUAD * (unit // 2 + 1))
                        for i in range(2):
                            j = 2 * jj + i
                            last = mm(ringA[:, job % 2, i, 0:n], Qz[:, unit % 2, j, qt * P:(qt + 1) * P],
                                      Ks[:, b, g, 0:n], True, l > 0)
                            if l == 0:
                                last = mm(ringA[:, job % 2, i, qt * P:(qt + 1) * P], identb[:, :], maskS[:, :],
                                          False, True)
                        last.then_inc(a_ready, 1)

                    def weigh():
                        e = s.t - 1
                        l, b, g = UNITS[e // TT]
                        kt = e % TT
                        q0 = span(l, kt)
                        pe.wait_ge(b_free, exps_before[e])
                        if kt == 0 and g == 0:
                            pe.wait_ge(b_free, v_job[l, b].bj + 2)
                        if kt == 0 and g % 2 == 0 and e >= 8:
                            pe.wait_ge(ctx_free, e // 8)
                        for j in range(QUAD):
                            last = mm(ctxP[PADD * j:PADD * (j + 1), q0:T], V[:, b, kt, QUAD * g + j, :],
                                      probs[:, QUAD * (e % 2) + j, q0:T], g % 2 == 0 and kt == 0,
                                      g % 2 == 1 and kt == TT - 1)
                        last.then_inc(pv_done, 1)

                    if s.e is not None:
                        score_t(0)
                        score_t(1)
                    if s.m is not None:
                        score(0)
                    if s.e is not None:
                        score_t(2)
                    if 1 <= s.t <= QUARTERS:
                        weigh()
                    if s.e is not None:
                        score_t(3)
                    if s.m is not None:
                        score(1)
                elif s.kind == "proj":
                    claim_a(s.a)
                    weights(s)
                    pe.wait_ge(norm_ok, 2 * TT * (s.n + 1))
                    for tt in range(TT):
                        o = ringA[:, s.a % 2, tt // 2, (tt % 2) * D:(tt % 2 + 1) * D]
                        for gg in range(2):
                            last = mm(o, ctxN[:, gg, tt * P:(tt + 1) * P], w_p[:, s.l, gg, :], gg == 0, gg == 1)
                    last.then_inc(a_ready, 1)
                elif s.kind == "spread":
                    pe.wait_ge(xhat_ok, s.n + 1)
                    for i, (c0, rows) in enumerate(((0, P), (P, REM))):
                        claim_b(s.bj + i)
                        for tt in range(TT):
                            last = nc.tensor.transpose(ringB[0:rows, (s.bj + i) % 3, tt * P:(tt + 1) * P],
                                                       xe[:, tt, c0:c0 + rows], ident[:, :])
                        last.then_inc(b_ready, 1)
                elif s.kind == "qk":
                    claim_a(s.a)
                    weights(s)
                    ln = ln_job[s.l, s.b, 0]
                    pe.wait_ge(b_free, ln.bj + 1)
                    pe.wait_ge(hrem_ok, ln.n + 1)
                    for i in range(2):
                        g = 2 * s.gp + i
                        mm(ringA[:, s.a % 2, i, :], w_qk[:, s.l % 2, s.side, g, :], hmain[:, :], True, False)
                        last = mm(ringA[:, s.a % 2, i, :], r_qk[:, s.l % 2, s.side, g, :], hrem[:, :], False, True)
                    last.then_inc(a_ready, 1)
                elif s.kind == "v":
                    for i in range(2):
                        claim_b(s.bj + i)
                        for k in range(2):
                            tt = 2 * i + k
                            o = ringB[:, (s.bj + i) % 3, k * D:(k + 1) * D]
                            mm(o, hmain[:, tt * P:(tt + 1) * P], w_v[:, s.l, :], True, False)
                            last = mm(o, hrem[:, tt * P:(tt + 1) * P], r_vw[:, s.l % 2, 0:D], False, True)
                        last.then_inc(b_ready, 1)
                elif s.kind == "w1":
                    ln = ln_job[s.l, s.b, 1]
                    weights(s)
                    pe.wait_ge(b_free, ln.bj + 1)
                    pe.wait_ge(hrem_ok, ln.n + 1)
                    for m in range(HT):
                        rows = P if m < HT - 1 else HLAST
                        claim_b(s.bj + m)
                        o = ringB[0:rows, (s.bj + m) % 3, :]
                        mm(o, w_1[:, s.l % 2, m * P:m * P + rows], hmain[:, :], True, False)
                        last = mm(o, r_vw[:, s.l % 2, D + m * P:D + m * P + rows], hrem[:, :], False, True)
                        last.then_inc(b_ready, 1)
                elif s.kind == "w2":
                    claim_a(s.a)
                    pe.wait_ge(b_free, w1_job[s.l, s.b].bj + HT)
                    for tt in range(TT):
                        o = ringA[:, s.a % 2, tt // 2, (tt % 2) * D:(tt % 2 + 1) * D]
                        for k in range(HT):
                            rows = P if k < HT - 1 else HLAST + 1
                            last = mm(o, hid[0:rows, k, tt * P:(tt + 1) * P], w_2[0:rows, s.l, k, :],
                                      k == 0, k == HT - 1)
                    last.then_inc(a_ready, 1)


def kernel(**inputs):
    import numpy as np
    import concourse.bacc as bacc
    from concourse.bass_utils import run_bass_kernel_spmd as run

    I = {name: np.asarray(a) for name, a in inputs.items()}
    none = np.zeros(3 * D, np.float32)
    qkv = [np.concatenate([I["L0_cond_W" + c] for c in "qkv"], 1), I["L1_cond_w_qkv"], I["L2_cond_W_qkv"],
           np.concatenate([I["L3_cond_w" + c] for c in "qkv"], 1)]
    b_qkv = [none, I["L1_cond_b_qkv"], I["L2_cond_b_qkv"], none]
    w1 = [I["L0_cond_W1"], I["L1_cond_w_fc1"], I["L2_cond_W_fc1"], I["L3_cond_fc1_w"]]
    b1 = [I["L0_cond_b1"], I["L1_cond_b_fc1"], I["L2_cond_b_fc1"], I["L3_cond_fc1_b"]]
    w2 = [I["L0_cond_W2"], I["L1_cond_w_fc2"], I["L2_cond_W_fc2"], I["L3_cond_fc2_w"]]
    b2 = [I["L0_cond_b2"], I["L1_cond_b_fc2"], I["L2_cond_b_fc2"], I["L3_cond_fc2_b"]]
    wp = [I["L0_cond_Wp"], I["L1_cond_w_proj"], I["L2_cond_W_proj"], I["L3_cond_wo"]]
    bp = [I["L0_cond_bp"], I["L1_cond_b_proj"], I["L2_cond_b_proj"], I["L3_cond_wo_b"]]
    wa = [I["L0_cond_Wa"], I["L1_cond_w_ada"], I["L2_cond_W_ada"], I["L3_cond_ada_w"]]
    ba = [I["L0_cond_ba"], I["L1_cond_b_ada"], I["L2_cond_b_ada"], I["L3_cond_ada_b"]]

    all1 = [np.concatenate([a, b], 1) for a, b in zip(qkv, w1)]
    bias1 = [np.concatenate([a, b]) for a, b in zip(b_qkv, b1)]
    w_main = np.stack([a[0:P] for a in all1])
    w_rem = np.stack([np.concatenate([a[P:D]] * 3 + [v[None]] * 2, 0) for a, v in zip(all1, bias1)])
    w_2 = np.zeros((LAYERS, P, HT, D), np.float32)
    w_p = np.zeros((LAYERS, P, 2, D), np.float32)
    ada_main = np.stack([a[0:P] for a in wa], 1)
    ada_rem = np.zeros((P, 6 * D), np.float32)
    c_rem = np.zeros((P, B), np.float32)
    for l in range(LAYERS):
        for k in range(HT):
            rows = w2[l][k * P:(k + 1) * P]
            w_2[l, 0:rows.shape[0], k] = rows
        w_2[l, HLAST, HT - 1] = b2[l]
        for h in range(HEADS):
            g, j = divmod(h, QUAD)
            at = PADD * j + HD * (g % 2)
            w_p[l, at:at + HD, g // 2] = wp[l][h * HD:(h + 1) * HD]
        w_p[l, SUM, 0] = bp[l]
        ada_rem[PADD * l:PADD * l + DREM] = wa[l][P:D]
        ada_rem[PADD * l + DREM] = ba[l]
        c_rem[PADD * l:PADD * l + DREM] = I["cond_1152"].T[P:D]
    thrice = [v * D + P + i for v in (0, 1, 3, 4) for _ in range(3) for i in range(DREM)]
    ln = np.stack([I["L3_cond_ln1_b"], I["L3_cond_ln1_w"], I["L3_cond_ln2_b"], I["L3_cond_ln2_w"]], 1)
    ln_rem = np.concatenate([ln[P:D]] * 3 + [np.zeros((2, 4), np.float32)], 0)

    consts = np.zeros((P, NC), np.float32)
    for j in range(QUAD):
        consts[PADD * j + 2 * HD:PADD * j + 3 * HD, 0] = -1.0
        consts[PADD * j + HD:PADD * j + 2 * HD, 1] = -1.0
    consts[2 * DREM:3 * DREM, 2] = -1.0
    consts[DREM:2 * DREM, 3] = -1.0
    consts[3 * DREM + 1, 3] = -1.0
    for l in range(LAYERS):
        consts[PADD * l:PADD * l + DREM, 4] = 1.0
        consts[PADD * l + DREM, 5] = 1.0
    kones = np.zeros((REM, PADD - SROWS), np.float32)
    kones[3 * DREM, 0:2] = 1.0
    modones = np.zeros((2, LAYERS, 4, B), np.float32)
    modones[:, :, 0::2, :] = 1.0

    nc = bacc.Bacc("TRN2", target_bir_lowering=False, num_devices=1)
    arrays, args = {}, {}
    for name, a in {"x": I["x"], "c_main": I["cond_1152"].T[0:P], "c_rem": c_rem, "ln_main": ln[0:P],
                    "ln_rem": ln_rem, "w_main": w_main, "w_rem": w_rem, "w_2": w_2, "w_p": w_p,
                    "ada_main": ada_main, "ada_rem": ada_rem,
                    "ada3_main": ada_main[:, :, thrice], "ada3_rem": ada_rem[:, thrice], "consts": consts, "kones": kones,
                    "modones": modones.reshape(2, LAYERS * 4 * B)}.items():
        a = np.ascontiguousarray(a)
        arrays[f"in_{name}"] = a
        args[name] = nc.dram_tensor(f"in_{name}", a.shape, mybir.dt.from_np(a.dtype), kind="ExternalInput").ap()
    out = nc.dram_tensor("out_x", (B, T, D), F32, kind="ExternalOutput").ap()
    program(nc, args, out)
    return run(nc, [arrays], core_ids=[0]).results[0]["out_x"]
```

```python
from contextlib import ExitStack

import concourse.bass as bass
from concourse import mybir

F32 = mybir.dt.float32
F32R = mybir.dt.float32r
BF16 = mybir.dt.bfloat16
ACT = mybir.ActivationFunctionType
ALU = mybir.AluOpType
AX_X = mybir.AxisListType.X

P = 128
LAYERS = 4
B, T, D = 2, 512, 144
HEADS = 16
HD = D // HEADS
HID = 4 * D
TT = T // P
QUAD = 4
GROUPS = HEADS // QUAD
DREM = D - P
REM = 3 * DREM + 2
SROWS = 3 * HD
MROW = SROWS
PADD = 32
SUM = 2 * HD
HT = -(-HID // P)
HLAST = HID - (HT - 1) * P
AT_MOST = {"copy": 1, "recip0": 2, "recip1": 2, "norm0": 4, "proj0": 5, "recip2": 4, "recip3": 4, "norm1": 4,
           "proj1": 6, "xhat": 8, "spread": 9, "w1": 10, "w20": 11, "w21": 11, "next_xhat": 14, "entry": 16,
           "stack": 28}
AT_LAST = {"copy": 1, "recip0": 1, "recip1": 1, "norm0": 1, "proj0": 3, "recip2": 1, "recip3": 1, "norm1": 1,
           "proj1": 3, "xhat": 3, "spread": 4, "w1": 5, "w20": 7, "w21": 7}
ENTRY = (1, 2, 2, 5, 8, 8, 10, 10, 6, 7)
GG0 = (1, 7, 6, 13, 9, 13, 14)
MOD, GATES = (6, 10, 15), (10, 12, 16, 20)
STACK1 = 28
FIRST_LEAD = 10
FIRST_REST, SECOND = -7, 2
SHIFT_AFTER = 1
PACE = (2, 0, 0, 0, 2, 0, 1, 1, 0, 2, 1, 2, 1, 1, 0, 2, 2, 1, 1, 2, 0, 1, 2, 2, 2, 1, 1, 0, 1, 1, 0, 0)
FIRST_PACE = (1, 1, 1, 2, 1, 1, 1, 1, 1, 1, 1, 1, 1, 1, 1, 1, 1, 1, 1, 1, 1, 1, 1, 1, 1, 1, 1, 1, 1, 1, 1, 1)
UNITS = [(l, b, g) for l in range(LAYERS) for b in range(B) for g in range(GROUPS)]
QUARTERS = TT * len(UNITS)
EPS = (1e-6, 1e-6, 1e-6, 1e-5)
MLP_FUNC = (ACT.Silu, ACT.Gelu_apprx_tanh, ACT.Gelu_apprx_tanh, ACT.Gelu)
NEG = -1e30
MODS = 4
NC = 8 + MODS * B
NR = 2 * GROUPS * P + D + HID
SCALE = HD ** -0.5


class Step:

    def __init__(self, kind, a, bj, n, l=0, b=0, half=0, side=0, gg=0, p=0, u=0, t=0, e=None, m=None):
        self.kind, self.a, self.bj, self.n = kind, a, bj, n
        self.l, self.b, self.half = l, b, half
        self.side, self.gg, self.p = side, gg, p
        self.u, self.t, self.e, self.m = u, t, e, m


def make_plan():
    plan = []
    jobs = {"a": 0, "b": 0}
    made = {}
    exps_last = set()

    def add(kind, a=0, bb=0, **k):
        plan.append(Step(kind, jobs["a"], jobs["b"], made.get(kind, 0), **k))
        jobs["a"] += a
        jobs["b"] += bb
        made[kind] = made.get(kind, 0) + 1
        if kind == "split":
            side = "split_k" if k["side"] else "split_q"
            made[side] = made.get(side, 0) + 1

    def chain(l, b):
        at = {}
        AT = AT_LAST if (l, b) == (LAYERS - 1, B - 1) else AT_MOST

        def put(key, kind, **k):
            at.setdefault(AT[key], []).append((kind, k))

        put("copy", "copy", b=b, gg=1)
        put("copy", "shuffle", gg=1)
        for p in range(TT):
            put(f"recip{p}", "recip", p=p)
            if p % 2:
                put(f"norm{p // 2}", "norm", l=l, b=b, gg=1, p=p // 2)
                put(f"proj{p // 2}", "proj", a=1, l=l, b=b, p=p // 2)
        put("xhat", "xhat", l=l, b=b, half=1)
        put("spread", "spread", bb=2, l=l, b=b, half=1)
        for m in range(HT):
            at.setdefault(AT["w1"] + m // 3, []).append(("w1", dict(bb=1, l=l, b=b, p=m)))
        exps_last.add(8 * GROUPS * (B * l + b + 1) + AT["w1"] + 1)
        for p in range(2):
            put(f"w2{p}", "w2", a=1, l=l, b=b, p=p)
        if l + 1 < LAYERS:
            put("next_xhat", "xhat", l=l + 1, b=b, half=0)
            for k, v in entry(l + 1, b).items():
                at.setdefault(AT["entry"] + k, []).extend(v)
        if b == B - 1 and l + 2 < LAYERS:
            put("stack", "stack", l=l + 2)
        return at

    def entry(l, b):
        at = {0: [("spread", dict(bb=2, l=l, b=b, half=0))]}
        for i, side in enumerate((0, 1) * GROUPS):
            at.setdefault(ENTRY[i], []).append(("qk", dict(bb=1, l=l, b=b, side=side, gg=i // 2)))
            at.setdefault(ENTRY[i] + 1, []).append(("split", dict(b=b, side=side, gg=i // 2)))
        for p in range(2):
            at.setdefault(ENTRY[8 + p], []).append(("v", dict(bb=1, l=l, b=b, p=p)))
        return at

    def place(first, pieces):
        for h, steps in pieces.items():
            dense.setdefault(first + h, []).extend(steps)

    dense = {}
    add("stats", b=0)
    add("mod", l=0)
    add("xhat", l=0, b=0, half=0)
    add("stack", l=0)
    first = entry(0, 0)
    for h in sorted(first):
        if h <= ENTRY[3] + 1:
            for kind, k in first[h]:
                add(kind, **k)
        else:
            dense.setdefault(h - ENTRY[3] + FIRST_REST, []).extend(first[h])
    for l in range(1, LAYERS):
        dense.setdefault(MOD[l - 1], []).append(("mod", dict(l=l)))
    for l in range(LAYERS):
        dense.setdefault(GATES[l], []).append(("gates", dict(a=1, l=l)))
    place(SECOND - 4, {0: [("stats", dict(b=1))]})
    place(SECOND - 1, {0: [("xhat", dict(l=0, b=1, half=0))]})
    place(STACK1, {0: [("stack", dict(l=1))]})
    place(SECOND, entry(0, 1))
    for l in range(LAYERS):
        for b in range(B):
            own = 8 * GROUPS * (B * l + b)
            place(own + 17, {0: [("copy", dict(b=b, gg=0))]})
            place(own + 17, {GG0[0]: [("shuffle", dict(gg=0))]})
            for p in range(TT):
                place(own + 17, {GG0[1 + p]: [("recip", dict(p=p))]})
                if p % 2:
                    place(own + 17, {GG0[5 + p // 2]: [("norm", dict(l=l, b=b, gg=0, p=p // 2))]})
            place(own + 32, chain(l, b))
    maxima = shifts = owed = 0
    for h in range(-FIRST_LEAD, max(max(dense) + 1, 2 * QUARTERS + 2)):
        t, p = h // 2, h % 2
        e = t if 0 <= t < QUARTERS else None
        exps = dict(bb=0 if e is None else 2, t=t, e=e, p=p)
        if (e is not None or h == 2 * QUARTERS + 1) and h not in exps_last:
            add("exp", **exps)
        if shifts < len(UNITS) and (maxima >= 8 * shifts + 8 + SHIFT_AFTER or h == 8 * shifts - 1):
            while maxima < 8 * shifts + 8:
                add("max", a=1, m=maxima // 2, p=maxima % 2)
                maxima += 1
                owed -= 1
            add("shift", a=1, u=shifts)
            shifts += 1
        pace = 1 if h < 0 else (FIRST_PACE if h < 32 else PACE)[h % 32]
        owed += pace
        ready = 8 * min(made.get("split_q", 0), made.get("split_k", 0))
        pace = max(0, min(owed, 2, ready - maxima, 2 * QUARTERS - maxima))
        owed -= pace
        pieces = [[] for _ in range(pace + 1)]
        for i, piece in enumerate(dense.get(h, [])):
            pieces[min(1 + i * pace // max(len(dense[h]), 1), pace)].append(piece)
        for i in range(pace + 1):
            if i:
                add("max", a=1, m=maxima // 2, p=maxima % 2)
                maxima += 1
            for kind, k in pieces[i]:
                add(kind, **k)
        if e is not None and h in exps_last:
            add("exp", **exps)
    return plan


def span(l, tile):
    return P * tile if l == 0 else 0


def program(nc, A, out):
    plan = make_plan()
    ctx = ExitStack()
    with ctx:
        def sb(name, shape, dt=F32):
            return ctx.enter_context(nc.sbuf_tensor(name, shape, dt))

        def sem(name):
            return ctx.enter_context(nc.semaphore(name))

        X = sb("X", [P, B * TT, D])
        w_qk = sb("w_qk", [P, 2, 2, GROUPS, P])
        w_v = sb("w_v", [P, LAYERS, D])
        w_1 = sb("w_1", [P, 2, HID])
        raw_r = sb("raw_r", [REM, NR])
        w_r = sb("w_r", [REM, 2, NR], F32R)
        w_2 = sb("w_2", [P, LAYERS, HT, D])
        w_p = sb("w_p", [P, LAYERS, 2, D])
        cB = sb("cB", [P, B, D])
        sB = sb("sB", [P, B, D + 1])
        cT = sb("cT", [P, B])
        cR = sb("cR", [P, B])
        sT = sb("sT", [P, B])
        sR = sb("sR", [P, B])
        sTb = sb("sTb", [P, B, P])
        sRb = sb("sRb", [P, B, P])
        mod = sb("mod", [P, LAYERS, MODS, B])
        modr = sb("modr", [REM, LAYERS, MODS, B])
        modn = sb("modn", [REM, LAYERS, MODS, B])
        lnw = sb("lnw", [P, 4])
        lnwr = sb("lnwr", [REM, 4])
        gate = sb("gate", [P, LAYERS, 2, B, D])
        consts = sb("consts", [P, NC])
        spare = sb("spare", [P, 1])
        ident = sb("ident", [P, P])
        identb = sb("identb", [P, P], BF16)
        maskS = sb("maskS", [P, P], BF16)
        maskT = sb("maskT", [P, P], BF16)
        half = sb("half", [P, TT])
        Qs = sb("Qs", [P, B, GROUPS, T], F32R)
        Ks = sb("Ks", [P, B, GROUPS, T], F32R)
        Qz = sb("Qz", [P, 2, QUAD, T], F32R)
        Kz = sb("Kz", [P, 2, QUAD, T], F32R)
        V = sb("V", [P, B, TT, HEADS, PADD])
        probs = sb("probs", [P, 2 * QUAD, T])
        NM = MODS * (D + 1)
        tmp_flat = sb("tmp", [P, NM])
        tmp = tmp_flat[:, 0:TT * D].rearrange("p (t d) -> p t d", d=D)
        part = sb("part", [P, 2, T], F32R)
        full = sb("full", [P, 2, T])
        nmr = sb("nmr", [P, TT])
        mx = sb("mx", [P, TT, QUAD])
        mrow = sb("mrow", [P, TT, P], BF16)
        ctxS = sb("ctxS", [P, T])
        ctxN = sb("ctxN", [P, 2, T])
        flat = ctxN[:, :, :].rearrange("p a b -> p (a b)")
        adar = flat[:, 0:2 * D]
        prods = (flat[:, 2 * D:2 * D + NM], tmp_flat[:, :])
        sums = sb("sums", [P, T])
        st = sb("st", [P, TT, 6])
        mv = sb("mv", [P, TT, 2])
        ve = sb("ve", [P, TT])
        rstd = sb("rstd", [P, TT])
        XE = 180
        xe = sb("xe", [P, TT, XE])
        hmain = sb("hmain", [P, T])
        yrem = sb("yrem", [REM, T])
        hrnd = sb("hrnd", [REM, T], F32R)
        hrem = sb("hrem", [REM, T], F32R)
        hid = sb("hid", [P, HT, T])
        adaT = hid[:, :, :].rearrange("p a b -> p (a b)")[:, 0:LAYERS * NM].rearrange("p (l n) -> p l n", l=LAYERS)
        adaT3 = [(probs[:, :, :] if l == 0 else w_2[:, l, :, :]).rearrange("p a b -> p (a b)")[0:3 * DREM, 0:NM]
                 for l in range(LAYERS)]
        gates_w = [w_1[:, 1, 0:2 * D]] + [
            w_qk[:, 1, :, :, :].rearrange("p a b c -> p (a b c)")[:, i * 2 * D:(i + 1) * 2 * D] for i in range(3)]

        ringA = ctx.enter_context(nc.psum_tensor("ringA", [P, 2, 2, T], F32))
        ringB = ctx.enter_context(nc.psum_tensor("ringB", [P, 3, T], F32))
        ctxP = ctx.enter_context(nc.psum_tensor("ctxP", [P, T], F32))

        small_in = sem("small_in")
        silu_in = sem("silu_in")
        x_in = [sem(f"x_in{b}") for b in range(B)]
        w_in = [sem(f"w_in{l}") for l in range(LAYERS)]
        raw_in = sem("raw_in")
        c_in = sem("c_in")
        ada_in = [sem(f"ada_in{l}") for l in range(LAYERS)]
        gate_in = sem("gate_in")
        prod_ok = sem("prod_ok")
        ones_ok = sem("ones_ok")
        prod_used = sem("prod_used")
        cleared = sem("cleared")
        consts_ok = sem("consts_ok")
        pool_ops = sem("pool_ops")
        dve_ops = sem("dve_ops")
        half_ok = sem("half_ok")
        silu_c = sem("silu_c")
        silu_b = sem("silu_b")
        mod_ok = sem("mod_ok")
        w_rounded = sem("w_rounded")
        w_ok = sem("w_ok")
        a_ready, a_free = sem("a_ready"), sem("a_free")
        b_ready, b_free = sem("b_ready"), sem("b_free")
        qk_ok = sem("qk_ok")
        xmain_ok = sem("xmain_ok")
        nmr_ok = sem("nmr_ok")
        qz_zero, kz_zero = sem("qz_zero"), sem("kz_zero")
        qz_in = [sem(f"qz_in{i}") for i in range(2)]
        kz_in = [sem(f"kz_in{i}") for i in range(2)]
        mrow_ok = sem("mrow_ok")
        pv_done = sem("pv_done")
        ctx_free = sem("ctx_free")
        recip_ok = sem("recip_ok")
        sums_ok = sem("sums_ok")
        norm_ok = sem("norm_ok")
        stats_ok = sem("stats_ok")
        rstd_ok = sem("rstd_ok")
        xhat_ok = sem("xhat_ok")
        hrem_ok = sem("hrem_ok")
        x_done = sem("x_done")
        stored = sem("stored")

        exps_before = {}
        for s in plan:
            if s.kind == "exp" and s.e is not None:
                exps_before[s.e] = s.bj + 2
        scores_before = {s.m: s.a + 1 for s in plan if s.kind == "max"}
        shift_job = {s.u: s.a for s in plan if s.kind == "shift"}
        qk_job = {(s.l, s.b, s.side, s.gg): s for s in plan if s.kind == "qk"}
        qk_done = {(s.l, s.b): s.bj + 1 for s in plan if s.kind == "qk"}
        v_done = {(s.l, s.b): s.bj + 1 for s in plan if s.kind == "v"}
        ln_job = {(s.l, s.b, s.half): s for s in plan if s.kind == "spread"}
        w1_done = {(s.l, s.b): s.bj + 1 for s in plan if s.kind == "w1"}
        normalised = {(s.l, s.b, s.half): s.n + 1 for s in plan if s.kind == "xhat"}
        norm_done = {(s.l, s.b, s.p): s.n + 1 for s in plan if s.kind == "norm" and s.gg == 1}
        gates_done = max(s.a + 1 for s in plan if s.kind == "gates")
        recips_before = []
        for i, s in enumerate(plan):
            if s.kind == "norm":
                recips_before.append(sum(r.kind == "recip" for r in plan[:i]))
        plan_xhat = [s for s in plan if s.kind == "xhat"]
        qk_steps = [s for s in plan if s.kind == "qk"]
        ln_steps = [s for s in plan if s.kind == "spread"]

        n_w = [0] * LAYERS
        n_ada = [0] * LAYERS
        n_raw = [0]
        n_gate = [0]
        n_c = [0]
        n_small = [0]
        n_silu = [0]
        block = ctx.enter_context(nc.Block())

        def load(eng, semaphore, dst, src, counter, i=0):
            eng.dma_start(dst, src).then_inc(semaphore, 16)
            counter[i] += 16

        def load_qkr(eng, l):
            if l >= 2:
                eng.wait_ge(b_ready, qk_done[l - 2, B - 1])
            if l > 0:
                eng.wait_ge(w_ok, l)
            load(eng, raw_in, raw_r[:, :], A["w_r"][l], n_raw)
            load(eng, w_in[l], w_qk[:, l % 2, :, :, :].rearrange("p s g c -> p (s g c)"), A["w_qk"][l], n_w, l)

        def load_w1(eng, l):
            if l >= 2:
                eng.wait_ge(b_ready, w1_done[l - 2, B - 1])
            load(eng, w_in[l], w_1[:, l % 2, :], A["w_1"][l], n_w, l)

        def load_rest(eng, l):
            load(eng, w_in[l], w_v[:, l, :], A["w_v"][l], n_w, l)
            load(eng, w_in[l], w_p[:, l, :, :], A["w_p"][l], n_w, l)
            load(eng, w_in[l], w_2[:, l, :, :], A["w_2"][l], n_w, l)

        def load_ada(eng, l):
            load(eng, ada_in[l], adaT[:, l, :], A["adaT_main"][l], n_ada, l)
            load(eng, ada_in[l], adaT3[l], A["adaT_rem"][l], n_ada, l)

        @block.sync
        def _(sp):
            x_v = A["x"].rearrange("b (t p) d -> p (b t) d", p=P)
            sp.dma_start(X[:, 0:TT, :], x_v[:, 0:TT, :]).then_inc(x_in[0], 16)
            load_ada(sp, 0)
            load(sp, small_in, consts[:, :], A["consts"], n_small)
            load(sp, small_in, modr[3 * DREM:REM, :, :, :].rearrange("p a b c -> p (a b c)"),
                 A["modones"], n_small)
            load_qkr(sp, 0)
            load(sp, silu_in, cT[:, :], A["c_main"], n_silu)
            load(sp, silu_in, cR[:, :], A["c_rem"], n_silu)
            load(sp, silu_in, lnw[:, :], A["ln_main"], n_silu)
            load(sp, silu_in, lnwr[:, :], A["ln_rem"], n_silu)
            sp.dma_start(X[:, TT:B * TT, :], x_v[:, TT:B * TT, :]).then_inc(x_in[1], 16)
            for l in range(1, LAYERS):
                load_ada(sp, l)
            for l in range(LAYERS):
                load(sp, gate_in, gates_w[l], A["ada_main"][l], n_gate)
            load(sp, gate_in, adar, A["ada_rem"], n_gate)
            load_rest(sp, 0)
            load_w1(sp, 0)

            def apart(what, u):
                l, b, g = UNITS[u]
                src, dst, sems, side = (Qs, Qz, qz_in, 0) if what == "q" else (Ks, Kz, kz_in, 1)
                sp.wait_ge(qk_ok, qk_job[l, b, side, g].n + 1)
                if u < 2:
                    sp.wait_ge(qz_zero if what == "q" else kz_zero, 1)
                elif what == "q":
                    sp.wait_ge(a_ready, scores_before[4 * (u - 2) + 3])
                else:
                    sp.wait_ge(b_ready, exps_before[4 * (u - 2) + 3])
                for j in range(QUAD):
                    rows = slice(PADD * j, PADD * (j + 1))
                    sp.dma_start(dst[rows, u % 2, j, :].bitcast(F32),
                                 src[rows, b, g, :].bitcast(F32)).then_inc(sems[u % 2], 16)

            requested = projected = stacked = 0
            moved = {"q": 0, "k": 0}
            split, used = {"q": 0, "k": 0}, {"q": 0, "k": 0}
            for s in plan:
                if s.kind == "split":
                    split["qk"[s.side]] += 1
                elif s.kind == "max" and s.m % TT == TT - 1 and s.p == 1:
                    used["q"] += 1
                elif s.kind == "exp" and s.e is not None and s.e % TT == TT - 1 and s.p == 1:
                    used["k"] += 1
                for what in "qk":
                    while moved[what] < min(split[what], used[what] + 2):
                        apart(what, moved[what])
                        moved[what] += 1
                if s.kind == "gates" and s.l == LAYERS - 1:
                    sp.wait_ge(a_ready, gates_done)
                    load_qkr(sp, 1)
                    load_w1(sp, 1)
                    requested = 2
                    for l in range(1, LAYERS):
                        sp.wait_ge(mod_ok, l + 1)
                        load_rest(sp, l)
                projected += s.kind == "qk" and s.b == B - 1 and s.gg == GROUPS - 1 and s.side == 1
                stacked += s.kind == "stack"
                if 2 <= requested < min(projected + 2, stacked + 1, LAYERS):
                    load_qkr(sp, requested)
                    requested += 1
                if s.kind == "w1" and s.b == B - 1 and s.p == HT - 1 and s.l + 2 < LAYERS:
                    load_w1(sp, s.l + 2)
            out_v = out.rearrange("b (t p) d -> p (b t) d", p=P)
            half_batch = TT // 2
            for i in range(2 * B):
                tiles = slice(i * half_batch, (i + 1) * half_batch)
                sp.wait_ge(x_done, i + 1)
                sp.dma_start(out_v[:, tiles, :], X[:, tiles, :]).then_inc(stored, 16)
            sp.wait_ge(stored, 2 * B * 16)

        @block.scalar
        def _(act):
            load(act, c_in, cB[:, :, :], A["c"].rearrange("b (a d) -> a b d", a=1).broadcast_to([P, B, D]), n_c)
            act.wait_ge(half_ok, 1)
            nc.scalar.activation(spare[:, :], half[:, 0:1], ACT.Silu)
            act.wait_ge(c_in, n_c[0])
            nc.scalar.activation(sB[:, :, 0:D], cB[:, :, :], ACT.Silu).then_inc(silu_c, 1)
            act.wait_ge(silu_in, n_silu[0])
            nc.scalar.activation(sT[:, :], cT[:, :], ACT.Silu).then_inc(silu_c, 1)
            nc.scalar.activation(sR[:, :], cR[:, :], ACT.Silu).then_inc(silu_c, 1)

            for s in plan:
                if s.kind == "exp" and s.e is not None:
                    l, b, g = UNITS[s.e // TT]
                    kt = s.e % TT
                    q0 = span(l, kt)
                    base = min(q0, T - 2 * P)
                    for i in range(2):
                        job = s.bj + i
                        j = 2 * s.p + i
                        act.wait_ge(b_ready, job + 1)
                        if s.e < 2 and j == 0:
                            act.wait_ge(mod_ok, 1)
                        if s.e >= 2:
                            act.wait_ge(pv_done, s.e - 1)
                        nc.scalar.activation(probs[:, QUAD * (s.e % 2) + j, q0:T],
                                             ringB[:, job % 3, q0 - base:T - base],
                                             ACT.Exp, scale=SCALE).then_inc(b_free, 1)
                elif s.kind == "spread":
                    v0 = 2 * s.half
                    act.wait_ge(mod_ok, s.l + 1)
                    act.wait_ge(b_ready, s.bj + 1)
                    nc.scalar.activation(hmain[:, :], ringB[:, s.bj % 3, :], ACT.Identity,
                                         scale=mod[:, s.l, v0 + 1, s.b:s.b + 1],
                                         bias=mod[:, s.l, v0, s.b:s.b + 1]).then_inc(b_free, 1)
                    act.wait_ge(b_ready, s.bj + 2)
                    if s.n >= 1:
                        act.wait_ge(hrem_ok, s.n)
                    for to, m in ((yrem, modr), (hrnd, modn)):
                        last = nc.scalar.activation(to[:, :], ringB[0:REM, (s.bj + 1) % 3, :], ACT.Identity,
                                                    scale=m[:, s.l, v0 + 1, s.b:s.b + 1],
                                                    bias=m[:, s.l, v0, s.b:s.b + 1])
                    last.then_inc(b_free, 1)
                elif s.kind == "stack":
                    act.wait_ge(raw_in, 16 * (s.l + 1))
                    if s.l >= 2:
                        act.wait_ge(b_ready, w1_done[s.l - 2, B - 1])
                    if s.l == 0:
                        act.wait_ge(small_in, n_small[0])
                    nc.scalar.activation(w_r[:, s.l % 2, :], raw_r[:, :], ACT.Identity,
                                         scale=consts[0:REM, 3:4]).then_inc(w_rounded, 1)
                elif s.kind == "qk":
                    act.wait_ge(b_ready, s.bj + 1)
                    if s.n >= 2:
                        act.wait_ge(qk_ok, s.n - 1)
                    nc.scalar.activation(part[:, s.n % 2, :], ringB[:, s.bj % 3, :], ACT.Identity,
                                         scale=consts[:, s.side:s.side + 1])
                    nc.scalar.activation(full[:, s.n % 2, :], ringB[:, s.bj % 3, :], ACT.Copy).then_inc(b_free, 1)
                elif s.kind == "copy":
                    act.wait_ge(pv_done, 8 * (s.n + 1))
                    if s.n:
                        act.wait_ge(norm_ok, 2 * s.n)
                    if s.n == 0:
                        act.wait_ge(mod_ok, LAYERS)
                    nc.scalar.activation(ctxS[:, :], ctxP[:, :], ACT.Copy).then_inc(ctx_free, 1)
                elif s.kind == "xhat":
                    act.wait_ge(nmr_ok, s.n + 1)
                    if s.n >= 1:
                        act.wait_ge(b_ready, ln_steps[s.n - 1].bj + 2)
                    for tt in range(TT):
                        last = nc.scalar.activation(xe[:, tt, 0:P], X[:, s.b * TT + tt, 0:P], ACT.Identity,
                                                    scale=rstd[:, tt:tt + 1], bias=nmr[:, tt:tt + 1])
                    last.then_inc(xmain_ok, 1)
                elif s.kind == "v":
                    act.wait_ge(b_ready, s.bj + 1)
                    if s.n == 0:
                        act.wait_ge(cleared, 1)
                    for k in range(2):
                        tt = 2 * s.p + k
                        for gg in range(2):
                            src = ringB[:, s.bj % 3, k * D + gg * 8 * HD:k * D + (gg + 1) * 8 * HD].rearrange(
                                "p (s j d) -> p s j d", s=2, j=QUAD)
                            for sx in range(2):
                                h0 = 8 * gg + QUAD * sx
                                last = nc.scalar.activation(V[:, s.b, tt, h0:h0 + QUAD, HD * sx:HD * sx + HD],
                                                            src[:, sx], ACT.Copy)
                    last.then_inc(b_free, 1)
                elif s.kind == "w1":
                    rows = P if s.p < HT - 1 else HLAST
                    act.wait_ge(b_ready, s.bj + 1)
                    if s.n == 0:
                        act.wait_ge(ones_ok, 1)
                    nc.scalar.activation(hid[0:rows, s.p, :], ringB[0:rows, s.bj % 3, :],
                                         MLP_FUNC[s.l]).then_inc(b_free, 1)

        def split_weights(engine, own, l):
            own.wait_ge(w_rounded, l + 1)
            engine.tensor_tensor(w_r[:, l % 2, :], w_r[:, l % 2, :].bitcast(F32), raw_r[:, :],
                                 ALU.add).then_inc(w_ok, 1)

        def normalise_context(engine, s):
            cols = slice(s.p * 2 * P, (s.p + 1) * 2 * P)
            engine.tensor_tensor(ctxN[:, s.gg, cols], ctxS[:, cols], sums[:, cols], ALU.mult).then_inc(norm_ok, 1)

        @block.gpsimd
        def _(pool):
            done = [0]

            def then(ins):
                done[0] += 1
                return ins.then_inc(pool_ops, 1)

            def settled():
                pool.wait_ge(pool_ops, done[0])

            nc.gpsimd.memset(half[:, :], -0.5).then_inc(half_ok, 1)
            then(nc.gpsimd.memset(xe[:, :, D + 2 * DREM:XE], 0.0))
            for m in (ident, identb, maskS, maskT):
                then(nc.gpsimd.memset(m[:, :], 0.0))
            settled()
            for m in (ident, identb):
                then(nc.gpsimd.affine_select(out=m[:, :], in_=m[:, :], compare_op=ALU.not_equal, fill=1.0,
                                             base=0, pattern=[[-1, P]], channel_multiplier=1))
            then(nc.gpsimd.affine_select(out=maskS[:, :], in_=maskS[:, :], compare_op=ALU.is_ge, fill=NEG,
                                         base=0, pattern=[[-1, P]], channel_multiplier=1))
            then(nc.gpsimd.affine_select(out=maskT[:, :], in_=maskT[:, :], compare_op=ALU.is_ge, fill=NEG,
                                         base=0, pattern=[[1, P]], channel_multiplier=-1))
            settled()
            nc.gpsimd.memset(sB[:, :, D:D + 1], 1.0).then_inc(consts_ok, 1)
            pool.wait_ge(consts_ok, 1)

            def products(l):
                pool.wait_ge(ada_in[l], n_ada[l])
                for b in range(B):
                    if l:
                        pool.wait_ge(prod_used, B * (l - 1) + b + 1)
                    s_b = sB[:, b, :].rearrange("p (a k) -> p a k", a=1).broadcast_to([P, MODS, D + 1])
                    nc.gpsimd.tensor_tensor(prods[b].rearrange("p (v k) -> p v k", v=MODS),
                                            adaT[:, l, :].rearrange("p (v k) -> p v k", v=MODS), s_b,
                                            ALU.mult).then_inc(prod_ok, 1)

            def power(s):
                pool.wait_ge(stats_ok, s.n + 1)
                if s.n >= 1:
                    pool.wait_ge(xhat_ok, s.n)
                    pool.wait_ge(xmain_ok, s.n)
                nc.gpsimd.tensor_tensor(rstd[:, :], ve[:, :], half[:, :], ALU.pow).then_inc(rstd_ok, 1)

            pool.wait_ge(silu_c, 1)
            products(0)
            before = [(prod_ok, B)]

            def alone():
                pool.wait_ge(*before[0])

            power(plan_xhat[0])
            pool.wait_ge(rstd_ok, 1)
            nc.gpsimd.memset(Qz[:, :, :, :].bitcast(F32), 0.0).then_inc(qz_zero, 1)
            before[0] = (qz_zero, 1)
            for s in plan:
                if s.kind == "xhat" and s.n >= 1:
                    alone()
                    power(s)
                    before[0] = (rstd_ok, s.n + 1)
                elif s.kind == "mod" and s.l >= 1:
                    alone()
                    products(s.l)
                    before[0] = (prod_ok, B * (s.l + 1))
                    if s.l == LAYERS - 1:
                        alone()
                        nc.gpsimd.memset(hid[HLAST:HLAST + 1, HT - 1, :], 1.0).then_inc(ones_ok, 1)
                        before[0] = (ones_ok, 1)
                elif s.kind == "spread" and s.n == 0:
                    alone()
                    then(nc.gpsimd.memset(V[:, :, :, :, HD:PADD], 0.0))
                    then(nc.gpsimd.memset(V[:, :, :, :, 0:HD], 0.0))
                    settled()
                    for b in range(B):
                        for sx in range(2):
                            v = V[:, b, :, :, SUM + sx:SUM + sx + 1].rearrange(
                                "p t (g s j) c -> p s (t g) (j c)", g=2, s=2)
                            then(nc.gpsimd.memset(v[:, sx], 1.0))
                    settled()
                    nc.gpsimd.memset(mrow[:, :, :], 0.0).then_inc(cleared, 1)
                    before[0] = (cleared, 1)
                elif s.kind == "split":
                    alone()
                    pool.wait_ge(b_free, qk_steps[s.n].bj + 1)
                    dst = (Ks if s.side else Qs)[:, s.b, s.gg, :]
                    nc.gpsimd.tensor_tensor(dst, part[:, s.n % 2, :].bitcast(F32), full[:, s.n % 2, :],
                                            ALU.add).then_inc(qk_ok, 1)
                    before[0] = (qk_ok, s.n + 1)
                elif s.kind == "stack" and s.l >= 1:
                    alone()
                    split_weights(nc.gpsimd, pool, s.l)
                    before[0] = (w_ok, s.l + 1)
                elif s.kind == "norm" and s.gg == 0:
                    alone()
                    pool.wait_ge(recip_ok, recips_before[s.n])
                    normalise_context(nc.gpsimd, s)
                    before[0] = (norm_ok, s.n + 1)

        @block.vector
        def _(dve):
            done = [0]

            def then(ins):
                done[0] += 1
                return ins.then_inc(dve_ops, 1)

            def settled():
                dve.wait_ge(dve_ops, done[0])

            nc.vector.memset(Kz[:, :, :, :].bitcast(F32), 0.0).then_inc(kz_zero, 1)

            def spread_silu():
                dve.wait_ge(silu_c, 3)
                then(nc.vector.tensor_scalar(sR[:, :], sR[:, :], consts[:, 4:5], consts[:, 5:6],
                                             ALU.mult, ALU.add))
                settled()
                for dst, src in ((sTb, sT), (sRb, sR)):
                    cols = src[:, :].rearrange("p (b a) -> p b a", a=1).broadcast_to([P, B, P])
                    if dst is sTb:
                        then(nc.vector.tensor_copy(dst[:, :, :], cols))
                    else:
                        nc.vector.tensor_copy(dst[:, :, :], cols).then_inc(silu_b, 1)

            def modulation(s):
                dve.wait_ge(ada_in[s.l], n_ada[s.l])
                if s.l == 0:
                    dve.wait_ge(silu_c, 1)
                    dve.wait_ge(consts_ok, 1)
                    dve.wait_ge(small_in, n_small[0])
                for b in range(B):
                    for i, buf in enumerate((ctxS, sums)):
                        n = 2 * (D + 1)
                        s_b = sB[0:3 * DREM, b, :].rearrange("p (a k) -> p a k", a=1).broadcast_to(
                            [3 * DREM, 2, D + 1])
                        then(nc.vector.tensor_tensor(
                            buf[0:3 * DREM, 0:n].rearrange("p (v k) -> p v k", v=2),
                            adaT3[s.l][:, i * n:(i + 1) * n].rearrange("p (v k) -> p v k", v=2), s_b, ALU.mult))
                        shares[i] = done[0]
                    for i, buf in enumerate((ctxS, sums)):
                        dve.wait_ge(dve_ops, shares[i])
                        then(nc.vector.tensor_reduce(
                            modr[0:3 * DREM, s.l, 2 * i:2 * i + 2, b],
                            buf[0:3 * DREM, 0:n].rearrange("p (v k) -> p v k", v=2), AX_X, ALU.add))
                    dve.wait_ge(prod_ok, B * s.l + b + 1)
                    nc.vector.tensor_reduce(
                        mod[:, s.l, :, b], prods[b].rearrange("p (v k) -> p v k", v=MODS),
                        AX_X, ALU.add).then_inc(prod_used, 1)
                    settled()
                dve.wait_ge(prod_used, B * (s.l + 1))
                plus = consts[:, 8:8 + MODS * B]
                for rows, dst in ((P, mod), (3 * DREM, modr)):
                    cols = dst[0:rows, s.l, :, :].rearrange("p v b -> p (v b)")
                    then(nc.vector.tensor_tensor(cols, cols, plus[0:rows, :], ALU.add))
                settled()
                if s.l == LAYERS - 1:
                    for dst, wb in ((mod, lnw), (modr[0:3 * DREM], lnwr[0:3 * DREM])):
                        for h in range(2):
                            sh, sc = dst[:, s.l, 2 * h, :], dst[:, s.l, 2 * h + 1, :]
                            then(nc.vector.scalar_tensor_tensor(out=sh, in0=sc, scalar=wb[:, 2 * h:2 * h + 1],
                                                                in1=sh, op0=ALU.mult, op1=ALU.add))
                            settled()
                            then(nc.vector.tensor_scalar(sc, sc, wb[:, 2 * h + 1:2 * h + 2], None, ALU.mult))
                    settled()
                nc.vector.tensor_scalar(modn[:, s.l, :, :], modr[:, s.l, :, :], consts[0:REM, 2:3], None,
                                        ALU.mult).then_inc(mod_ok, 1)

            def statistics(b, tiles):
                for tt in tiles:
                    then(nc.vector.bn_stats(st[:, tt, :], X[:, b * TT + tt, :]))

            def aggregate(tiles):
                for tt in tiles:
                    then(nc.vector.bn_aggr(mv[:, tt, :], st[:, tt, :]))

            def variances(l):
                nc.vector.tensor_scalar(ve[:, :], mv[:, :, 1], EPS[l], None, ALU.add).then_inc(stats_ok, 1)

            def normalise(s):
                dve.wait_ge(rstd_ok, s.n + 1)
                if s.n >= 1:
                    dve.wait_ge(xmain_ok, s.n)
                nc.vector.scalar_tensor_tensor(out=nmr[:, :], in0=mv[:, :, 0], scalar=-1.0, in1=rstd[:, :],
                                               op0=ALU.mult, op1=ALU.mult).then_inc(nmr_ok, 1)
                if s.n >= 1:
                    dve.wait_ge(b_ready, ln_steps[s.n - 1].bj + 2)
                for tt in range(TT):
                    x = X[:, s.b * TT + tt, P:D].rearrange("p (a c) -> p a c", a=1).broadcast_to([P, 3, DREM])
                    last = nc.vector.tensor_scalar(
                        xe[:, tt, P:P + 3 * DREM].rearrange("p (a c) -> p a c", a=3), x,
                        mv[:, tt, 0:1], rstd[:, tt:tt + 1], ALU.subtract, ALU.mult)
                    if tt < TT - 1:
                        then(last)
                last.then_inc(xhat_ok, 1)

            def residual(s, h):
                tiles = (2 * s.p, 2 * s.p + 1)
                last_use = h == 1 and s.l == LAYERS - 1
                xs = X[:, s.b * TT + tiles[0]:s.b * TT + tiles[0] + 2, :]
                if h == 0 and s.p == 0:
                    dve.wait_ge(a_free, gates_done)
                part_ = tmp[:, tiles[0]:tiles[0] + 2, :]
                g = gate[:, s.l, h, s.b, :].rearrange("p (a d) -> p a d", a=1).broadcast_to([P, 2, D])
                dve.wait_ge(a_ready, s.a + 1)
                nc.vector.tensor_tensor(part_, ringA[:, s.a % 2, 0, 0:2 * D].rearrange("p (a d) -> p a d", d=D), g,
                                        ALU.mult).then_inc(a_free, 1)
                if s.p == 1 and not last_use:
                    dve.wait_ge(dve_ops, added[0])
                    statistics(s.b, (0, 1))
                    first = done[0]
                dve.wait_ge(a_free, s.a + 1)
                dve.wait_ge(xmain_ok, normalised[s.l, s.b, h])
                add = nc.vector.tensor_tensor(xs, xs, part_, ALU.add)
                if last_use:
                    add.then_inc(x_done, 1)
                    return
                then(add)
                added[0] = done[0]
                if s.p == 1:
                    dve.wait_ge(dve_ops, first)
                    aggregate((0, 1))
                    dve.wait_ge(dve_ops, added[0])
                    statistics(s.b, tiles)
                    settled()
                    aggregate(tiles)
                    settled()
                    variances(s.l + h)

            shares = [0, 0]
            added = [0]
            shuffled = [0]
            for s in plan:
                if s.kind == "stats":
                    dve.wait_ge(x_in[s.b], 16)
                    if s.n > 0:
                        dve.wait_ge(xhat_ok, s.n)
                    statistics(s.b, range(TT))
                    settled()
                    aggregate(range(TT))
                    settled()
                    variances(0)
                elif s.kind == "mod":
                    modulation(s)
                elif s.kind == "gates":
                    dve.wait_ge(a_ready, s.a + 1)
                    to = gate[:, s.l, :, :, :].rearrange("p h b d -> p (h b d)")
                    then(nc.vector.tensor_copy(to[:, 0:3 * D], ringA[:, s.a % 2, 0, 0:3 * D]))
                    nc.vector.tensor_copy(to[:, 3 * D:4 * D], ringA[:, s.a % 2, 1, 0:D]).then_inc(a_free, 1)
                    settled()
                elif s.kind == "stack":
                    if s.l == 0:
                        spread_silu()
                        split_weights(nc.vector, dve, 0)
                elif s.kind == "max":
                    l, b, g = UNITS[s.m // TT]
                    qt = s.m % TT
                    n = P * (qt + 1) if l == 0 else T
                    if s.m == 0:
                        dve.wait_ge(cleared, 1)
                    dve.wait_ge(a_ready, s.a + 1)
                    if qt == 0 and s.p == 0 and s.m >= TT:
                        dve.wait_ge(mrow_ok, s.m // TT)
                    nc.vector.reduce_max(mx[:, qt, 2 * s.p:2 * s.p + 2], ringA[:, s.a % 2, :, 0:n],
                                         AX_X).then_inc(a_free, 1)
                    if qt == TT - 1 and s.p == 1:
                        dve.wait_ge(a_free, s.a + 1)
                        if s.m // TT >= 1:
                            dve.wait_ge(a_ready, shift_job[s.m // TT - 1] + 1)
                        cols = mrow[:, :, :].rearrange("p t (j c) -> p t j c", c=PADD)
                        then(nc.vector.tensor_scalar(cols[:, :, :, MROW], mx[:, :, :], -1.0, None, ALU.mult))
                        settled()
                        nc.vector.scalar_tensor_tensor(out=cols[:, :, :, MROW + 1], in0=mx[:, :, :], scalar=-1.0,
                                                       in1=cols[:, :, :, MROW], op0=ALU.mult,
                                                       op1=ALU.subtract).then_inc(mrow_ok, 1)
                elif s.kind == "shift":
                    l, b, g = UNITS[s.u]
                    dve.wait_ge(a_ready, s.a + 1)
                    nc.vector.tensor_tensor(Qs[:, b, g, :], ringA[:, s.a % 2, 0, :], Qs[:, b, g, :].bitcast(F32),
                                            ALU.add).then_inc(a_free, 1)
                elif s.kind == "xhat":
                    normalise(s)
                elif s.kind == "spread":
                    dve.wait_ge(b_free, s.bj + 2)
                    nc.vector.tensor_tensor(hrem[:, :], hrnd[:, :].bitcast(F32), yrem[:, :],
                                            ALU.add).then_inc(hrem_ok, 1)
                elif s.kind == "shuffle":
                    dve.wait_ge(ctx_free, s.n + 1)
                    if s.n:
                        dve.wait_ge(norm_ok, 2 * s.n)
                    mask = [SUM + 1 if HD <= i < 2 * HD or i == SUM + 1 else SUM for i in range(PADD)]
                    nc.vector.stream_shuffle(sums[:, :], ctxS[:, :], mask).then_inc(sums_ok, 1)
                    shuffled[0] = s.n + 1
                elif s.kind == "recip":
                    cols = slice(s.p * P, (s.p + 1) * P)
                    dve.wait_ge(sums_ok, shuffled[0])
                    nc.vector.reciprocal(sums[:, cols], sums[:, cols]).then_inc(recip_ok, 1)
                elif s.kind == "norm" and s.gg == 1:
                    dve.wait_ge(recip_ok, recips_before[s.n])
                    normalise_context(nc.vector, s)
                elif s.kind == "proj":
                    residual(s, 0)
                elif s.kind == "w2":
                    residual(s, 1)

        @block.tensor
        def _(pe):
            def mm(out_, lhsT, rhs, start, stop):
                return nc.tensor.matmul(out_, lhsT, rhs, start=start, stop=stop)

            def claim_a(job):
                if job >= 2:
                    pe.wait_ge(a_free, job - 1)

            def claim_b(job):
                if job >= 3:
                    pe.wait_ge(b_free, job - 2)

            C_V = 2 * GROUPS * P
            C_1 = C_V + D

            def weights(s):
                pe.wait_ge(w_in[s.l], n_w[s.l])

            def remainder(s, ln):
                pe.wait_ge(w_ok, s.l + 1)
                pe.wait_ge(hrem_ok, ln.n + 1)

            for s in plan:
                if s.kind == "gates":
                    claim_a(s.a)
                    pe.wait_ge(gate_in, n_gate[0])
                    pe.wait_ge(silu_b, 1)
                    rows = slice(PADD * s.l, PADD * s.l + DREM + 1)
                    for h in range(2):
                        for b in range(B):
                            k, at = divmod(h * B + b, 3)
                            o = ringA[:, s.a % 2, k, at * D:(at + 1) * D]
                            mm(o, sTb[:, b, :], gates_w[s.l][:, h * D:(h + 1) * D], True, False)
                            last = mm(o, sRb[rows, b, :], adar[rows, h * D:(h + 1) * D], False, True)
                    last.then_inc(a_ready, 1)
                elif s.kind == "shift":
                    claim_a(s.a)
                    pe.wait_ge(mrow_ok, s.u + 1)
                    for qt in range(TT):
                        last = mm(ringA[:, s.a % 2, 0, qt * P:(qt + 1) * P], mrow[:, qt, :], identb[:, :], True, True)
                    last.then_inc(a_ready, 1)
                elif s.kind == "exp":
                    def score_t(i):
                        l, b, g = UNITS[s.e // TT]
                        j = 2 * s.p + i
                        kt = s.e % TT
                        job = s.bj + i
                        unit = s.e // TT
                        q0 = span(l, kt)
                        base = min(q0, T - 2 * P)
                        claim_b(job)
                        if kt == 0 and j == 0:
                            pe.wait_ge(a_free, shift_job[unit] + 1)
                            pe.wait_ge(kz_in[unit % 2], 16 * QUAD * (unit // 2 + 1))
                        last = mm(ringB[:, job % 3, 0:T - base], Kz[:, unit % 2, j, kt * P:(kt + 1) * P],
                                  Qs[:, b, g, base:T], True, l > 0)
                        if l == 0:
                            last = mm(ringB[:, job % 3, q0 - base:q0 - base + P], identb[:, :], maskT[:, :],
                                      False, True)
                        last.then_inc(b_ready, 1)

                    def weigh():
                        e = s.t - 1
                        l, b, g = UNITS[e // TT]
                        kt = e % TT
                        q0 = span(l, kt)
                        pe.wait_ge(b_free, exps_before[e])
                        if kt == 0 and g == 0:
                            pe.wait_ge(b_free, v_done[l, b])
                        if kt == 0 and g % 2 == 0 and e >= 8:
                            pe.wait_ge(ctx_free, e // 8)
                        for j in range(QUAD):
                            last = mm(ctxP[PADD * j:PADD * (j + 1), q0:T], V[:, b, kt, QUAD * g + j, :],
                                      probs[:, QUAD * (e % 2) + j, q0:T], g % 2 == 0 and kt == 0,
                                      g % 2 == 1 and kt == TT - 1)
                        last.then_inc(pv_done, 1)

                    if s.e is not None:
                        score_t(0)
                    if s.p == 1 and s.t >= 1:
                        weigh()
                    if s.e is not None:
                        score_t(1)
                elif s.kind == "max":
                    l, b, g = UNITS[s.m // TT]
                    qt = s.m % TT
                    unit = s.m // TT
                    n = max(P * (qt + 1), 2 * P) if l == 0 else T
                    claim_a(s.a)
                    if qt == 0 and s.p == 0:
                        pe.wait_ge(qk_ok, qk_job[l, b, 1, g].n + 1)
                        pe.wait_ge(qz_in[unit % 2], 16 * QUAD * (unit // 2 + 1))
                    for i in range(2):
                        j = 2 * s.p + i
                        last = mm(ringA[:, s.a % 2, i, 0:n], Qz[:, unit % 2, j, qt * P:(qt + 1) * P],
                                  Ks[:, b, g, 0:n], True, l > 0)
                        if l == 0:
                            last = mm(ringA[:, s.a % 2, i, qt * P:(qt + 1) * P], identb[:, :], maskS[:, :],
                                      False, True)
                    last.then_inc(a_ready, 1)
                elif s.kind == "proj":
                    claim_a(s.a)
                    weights(s)
                    pe.wait_ge(norm_ok, norm_done[s.l, s.b, s.p])
                    for k in range(2):
                        tt = 2 * s.p + k
                        o = ringA[:, s.a % 2, 0, k * D:(k + 1) * D]
                        for gg in range(2):
                            last = mm(o, ctxN[:, gg, tt * P:(tt + 1) * P], w_p[:, s.l, gg, :], gg == 0, gg == 1)
                    last.then_inc(a_ready, 1)
                elif s.kind == "spread":
                    if s.n == 0:
                        pe.wait_ge(consts_ok, 1)
                    pe.wait_ge(xmain_ok, s.n + 1)
                    for i, (c0, rows) in enumerate(((0, P), (P, REM))):
                        claim_b(s.bj + i)
                        if i:
                            pe.wait_ge(xhat_ok, s.n + 1)
                        for tt in range(TT):
                            last = nc.tensor.transpose(ringB[0:rows, (s.bj + i) % 3, tt * P:(tt + 1) * P],
                                                       xe[:, tt, c0:c0 + rows], ident[:, :])
                        last.then_inc(b_ready, 1)
                elif s.kind == "qk":
                    claim_b(s.bj)
                    weights(s)
                    ln = ln_job[s.l, s.b, 0]
                    pe.wait_ge(b_free, ln.bj + 1)
                    mm(ringB[:, s.bj % 3, :], w_qk[:, s.l % 2, s.side, s.gg, :], hmain[:, :], True, False)
                    remainder(s, ln)
                    at = (GROUPS * s.side + s.gg) * P
                    mm(ringB[:, s.bj % 3, :], w_r[:, s.l % 2, at:at + P], hrem[:, :], False, True).then_inc(b_ready, 1)
                elif s.kind == "v":
                    claim_b(s.bj)
                    for k in range(2):
                        tt = 2 * s.p + k
                        o = ringB[:, s.bj % 3, k * D:(k + 1) * D]
                        mm(o, hmain[:, tt * P:(tt + 1) * P], w_v[:, s.l, :], True, False)
                        last = mm(o, hrem[:, tt * P:(tt + 1) * P], w_r[:, s.l % 2, C_V:C_V + D], False, True)
                    last.then_inc(b_ready, 1)
                elif s.kind == "w1":
                    ln = ln_job[s.l, s.b, 1]
                    weights(s)
                    pe.wait_ge(b_free, ln.bj + 1)
                    m = s.p
                    rows = P if m < HT - 1 else HLAST
                    claim_b(s.bj)
                    o = ringB[0:rows, s.bj % 3, :]
                    mm(o, w_1[:, s.l % 2, m * P:m * P + rows], hmain[:, :], True, False)
                    remainder(s, ln)
                    last = mm(o, w_r[:, s.l % 2, C_1 + m * P:C_1 + m * P + rows], hrem[:, :], False, True)
                    last.then_inc(b_ready, 1)
                elif s.kind == "w2":
                    claim_a(s.a)
                    pe.wait_ge(ones_ok, 1)
                    pe.wait_ge(b_free, w1_done[s.l, s.b])
                    for i in range(2):
                        tt = 2 * s.p + i
                        o = ringA[:, s.a % 2, 0, i * D:(i + 1) * D]
                        for k in range(HT):
                            rows = P if k < HT - 1 else HLAST + 1
                            last = mm(o, hid[0:rows, k, tt * P:(tt + 1) * P], w_2[0:rows, s.l, k, :],
                                      k == 0, k == HT - 1)
                    last.then_inc(a_ready, 1)


def kernel(**inputs):
    import numpy as np
    import concourse.bacc as bacc
    from concourse.bass_utils import run_bass_kernel_spmd as run

    I = {name: np.asarray(a) for name, a in inputs.items()}
    none = np.zeros(3 * D, np.float32)
    qkv = [np.concatenate([I["L0_cond_W" + c] for c in "qkv"], 1), I["L1_cond_w_qkv"], I["L2_cond_W_qkv"],
           np.concatenate([I["L3_cond_w" + c] for c in "qkv"], 1)]
    b_qkv = [none, I["L1_cond_b_qkv"], I["L2_cond_b_qkv"], none]
    w1 = [I["L0_cond_W1"], I["L1_cond_w_fc1"], I["L2_cond_W_fc1"], I["L3_cond_fc1_w"]]
    b1 = [I["L0_cond_b1"], I["L1_cond_b_fc1"], I["L2_cond_b_fc1"], I["L3_cond_fc1_b"]]
    w2 = [I["L0_cond_W2"], I["L1_cond_w_fc2"], I["L2_cond_W_fc2"], I["L3_cond_fc2_w"]]
    b2 = [I["L0_cond_b2"], I["L1_cond_b_fc2"], I["L2_cond_b_fc2"], I["L3_cond_fc2_b"]]
    wp = [I["L0_cond_Wp"], I["L1_cond_w_proj"], I["L2_cond_W_proj"], I["L3_cond_wo"]]
    bp = [I["L0_cond_bp"], I["L1_cond_b_proj"], I["L2_cond_b_proj"], I["L3_cond_wo_b"]]
    wa = [I["L0_cond_Wa"], I["L1_cond_w_ada"], I["L2_cond_W_ada"], I["L3_cond_ada_w"]]
    ba = [I["L0_cond_ba"], I["L1_cond_b_ada"], I["L2_cond_b_ada"], I["L3_cond_ada_b"]]

    def stack(w):
        s = np.zeros((w.shape[0], HEADS, PADD), w.dtype)
        s[:, :, 0:SROWS] = np.tile(w.reshape(-1, HEADS, HD), (1, 1, 3))
        return s.reshape(-1, HEADS * PADD)

    w_qk = np.stack([np.concatenate([stack(a[0:P, 0:D]), stack(a[0:P, D:2 * D])], 1) for a in qkv])
    w_r = []
    for a, w, bq, bw in zip(qkv, w1, b_qkv, b1):
        full = np.concatenate([a[P:D]] * 3 + [bq[None]] * 2, 0)
        k = stack(full[:, D:2 * D])
        k.reshape(REM, HEADS, PADD)[3 * DREM:, :, SROWS:SROWS + 2] = 1.0
        w_r.append(np.concatenate([stack(full[:, 0:D]), k, full[:, 2 * D:],
                                   np.concatenate([w[P:D]] * 3 + [bw[None]] * 2, 0)], 1))
    w_r = np.stack(w_r)
    w_v = np.stack([a[0:P, 2 * D:] for a in qkv])
    w_1 = np.stack([w[0:P] for w in w1])
    w_2 = np.zeros((LAYERS, P, HT, D), np.float32)
    w_p = np.zeros((LAYERS, P, 2, D), np.float32)
    both = [np.concatenate([a, v[None]], 0).reshape(D + 1, 6, D) for a, v in zip(wa, ba)]
    adaT = np.stack([a[:, [0, 1, 3, 4]].transpose(2, 1, 0).reshape(D, MODS * (D + 1)) for a in both])
    gates = np.stack([a[:, [2, 5]].reshape(D + 1, 2 * D) for a in both])
    ada_rem = np.zeros((P, 2 * D), np.float32)
    c_rem = np.zeros((P, B), np.float32)
    for l in range(LAYERS):
        for k in range(HT):
            rows = w2[l][k * P:(k + 1) * P]
            w_2[l, 0:rows.shape[0], k] = rows
        w_2[l, HLAST, HT - 1] = b2[l]
        for h in range(HEADS):
            g, j = divmod(h, QUAD)
            at = PADD * j + HD * (g % 2)
            w_p[l, at:at + HD, g // 2] = wp[l][h * HD:(h + 1) * HD]
        w_p[l, SUM, 0] = bp[l]
        ada_rem[PADD * l:PADD * l + DREM + 1] = gates[l, P:]
        c_rem[PADD * l:PADD * l + DREM] = I["cond_1152"].T[P:D]
    ln = np.stack([I["L3_cond_ln1_b"], I["L3_cond_ln1_w"], I["L3_cond_ln2_b"], I["L3_cond_ln2_w"]], 1)
    ln_rem = np.concatenate([ln[P:D]] * 3 + [np.zeros((2, 4), np.float32)], 0)

    consts = np.zeros((P, NC), np.float32)
    for j in range(QUAD):
        consts[PADD * j + 2 * HD:PADD * j + 3 * HD, 0] = -1.0
        consts[PADD * j + HD:PADD * j + 2 * HD, 1] = -1.0
    consts[2 * DREM:3 * DREM, 2] = -1.0
    consts[DREM:2 * DREM, 3] = -1.0
    consts[3 * DREM + 1, 3] = -1.0
    for l in range(LAYERS):
        consts[PADD * l:PADD * l + DREM, 4] = 1.0
        consts[PADD * l + DREM, 5] = 1.0
    consts[:, 8:].reshape(P, MODS, B)[:, 1::2] = 1.0
    modones = np.zeros((2, LAYERS, MODS, B), np.float32)
    modones[:, :, 0::2, :] = 1.0

    nc = bacc.Bacc("TRN2", target_bir_lowering=False, num_devices=1)
    arrays, args = {}, {}
    for name, a in {"x": I["x"], "c_main": I["cond_1152"].T[0:P], "c_rem": c_rem, "ln_main": ln[0:P],
                    "ln_rem": ln_rem, "w_qk": w_qk, "w_r": w_r, "w_v": w_v, "w_1": w_1, "w_2": w_2, "w_p": w_p,
                    "ada_main": gates[:, 0:P], "ada_rem": ada_rem, "adaT_main": adaT[:, 0:P],
                    "adaT_rem": np.concatenate([adaT[:, P:]] * 3, 1), "c": I["cond_1152"], "consts": consts,
                    "modones": modones.reshape(2, LAYERS * MODS * B)}.items():
        a = np.ascontiguousarray(a)
        arrays[f"in_{name}"] = a
        args[name] = nc.dram_tensor(f"in_{name}", a.shape, mybir.dt.from_np(a.dtype), kind="ExternalInput").ap()
    out = nc.dram_tensor("out_x", (B, T, D), F32, kind="ExternalOutput").ap()
    program(nc, args, out)
    return run(nc, [arrays], core_ids=[0]).results[0]["out_x"]
```
